# Optimizing a Trainium2 kernel written in Bass

```python
import numpy as np
import jax
import jax.numpy as jnp

def _softmax(x, axis=-1):
    return jax.nn.softmax(x, axis=axis)

def _gelu(x):
    return jax.nn.gelu(x, approximate=True)

def _silu(x):
    return jax.nn.silu(x)

def _sigmoid(x):
    return jax.nn.sigmoid(x)

def _layernorm(x, axis=-1, eps=1e-05):
    m = jnp.mean(x, axis=axis, keepdims=True)
    v = jnp.var(x, axis=axis, keepdims=True)
    return (x - m) / jnp.sqrt(v + eps)

def _scatter_add(tgt, idx, src, axis=0):
    return tgt.at[idx].add(src)

def _segment_sum(src, seg, n):
    return jax.ops.segment_sum(src, seg, n)
kernel_name = 'mk_xattn_seq_d1_seqx_r2_71ac46'

def setup_inputs(seed: int=0):
    np.random.seed(seed)
    _w = jnp.asarray

    def _rec_inputs():
        import jax
        import jax.numpy as jnp
        _rk = jax.random.key(seed)
        x = 7.22e-05 + 1 * jax.random.normal(jax.random.fold_in(_rk, 1), (16, 1024, 512), jnp.float32)
        _lenS = 1024 - jax.random.randint(jax.random.fold_in(_rk, 7), (16,), 0, max(1, 1024 // 4) + 1, jnp.int32)
        _lenS2 = 64 - jax.random.randint(jax.random.fold_in(_rk, 8), (16,), 0, max(1, 64 // 4) + 1, jnp.int32)
        _ctx_1024P = jax.random.normal(jax.random.fold_in(_rk, 11), (16, 16, 512), jnp.float32)
        _ctx_1024c = jax.random.dirichlet(jax.random.fold_in(_rk, 511), 0.3 * jnp.ones((16,), jnp.float32), (16, 64))
        _ctx_1024t = jnp.einsum('bsk,bkd->bsd', _ctx_1024c, _ctx_1024P)
        _ctx_1024t = _ctx_1024t * jax.lax.rsqrt(jnp.mean(jnp.square(_ctx_1024t)) + 1e-12) * 0.953939
        ctx_1024 = 4.13588e-05 + 0.999923 * (_ctx_1024t + 0.3 * jax.random.normal(jax.random.fold_in(_rk, 611), (16, 64, 512), jnp.float32))
        _validS = jnp.arange(1024)[None, :] < _lenS[:, None]
        _validS2 = jnp.arange(64)[None, :] < _lenS2[:, None]
        _causal = jnp.tril(jnp.ones((1024, 1024), dtype=bool))
        mask_BxSxS2_ik1 = jnp.where(jnp.broadcast_to(_validS2[:, None, :], (16, 1024, 64)), 1, 0).astype(jnp.int32)
        return (x, ctx_1024, mask_BxSxS2_ik1)
    x, ctx_1024, mask_BxSxS2_ik1 = _rec_inputs()

    def _L0_xattn_setup():
        import jax, jax.numpy as jnp
        import numpy as np
        B, T, D, H, DK = (4, 1024, 512, 16, 64)
        key = jax.random.key(seed)
        ks = jax.random.split(key, 9)
        s = 0.02
        return {'q': jax.random.normal(ks[0], (B, T, D), jnp.float32), 'k': jax.random.normal(ks[1], (B, T, D), jnp.float32), 'v': jax.random.normal(ks[2], (B, T, D), jnp.float32), 'attn_mask': jax.random.randint(ks[3], (B, T, T), 0, 2, jnp.int32), 'Wq': jax.random.normal(ks[4], (D, H * DK), jnp.float32) * s, 'bq': jnp.zeros((H * DK,), jnp.float32), 'Wk': jax.random.normal(ks[5], (D, H * DK), jnp.float32) * s, 'bk': jnp.zeros((H * DK,), jnp.float32), 'Wv': jax.random.normal(ks[6], (D, H * DK), jnp.float32) * s, 'bv': jnp.zeros((H * DK,), jnp.float32), 'Wo': jax.random.normal(ks[7], (H * DK, D), jnp.float32) * s, 'bo': jnp.zeros((D,), jnp.float32), 'gamma': jnp.ones((D,), jnp.float32), 'beta': jnp.zeros((D,), jnp.float32)}
    _L0_xattn_all = _L0_xattn_setup()
    _L0_xattn_in = {k: v for k, v in _L0_xattn_all.items() if k in ('Wq', 'bq', 'Wk', 'bk', 'Wv', 'bv', 'Wo', 'bo', 'gamma', 'beta')}
    del _L0_xattn_all
    return {'x': x, 'ctx_1024': ctx_1024, 'mask_BxSxS2_ik1': mask_BxSxS2_ik1, 'L0_xattn_Wq': _L0_xattn_in['Wq'], 'L0_xattn_bq': _L0_xattn_in['bq'], 'L0_xattn_Wk': _L0_xattn_in['Wk'], 'L0_xattn_bk': _L0_xattn_in['bk'], 'L0_xattn_Wv': _L0_xattn_in['Wv'], 'L0_xattn_bv': _L0_xattn_in['bv'], 'L0_xattn_Wo': _L0_xattn_in['Wo'], 'L0_xattn_bo': _L0_xattn_in['bo'], 'L0_xattn_gamma': _L0_xattn_in['gamma'], 'L0_xattn_beta': _L0_xattn_in['beta']}

def reference(x, ctx_1024, mask_BxSxS2_ik1, L0_xattn_Wq, L0_xattn_bq, L0_xattn_Wk, L0_xattn_bk, L0_xattn_Wv, L0_xattn_bv, L0_xattn_Wo, L0_xattn_bo, L0_xattn_gamma, L0_xattn_beta):
    import jax
    import jax.numpy as jnp

    def _L0_xattn_ref(q, k, v, attn_mask, Wq, bq, Wk, bk, Wv, bv, Wo, bo, gamma, beta):
        import jax, jax.numpy as jnp
        import numpy as np
        B, T, D, H, DK = (4, 1024, 512, 16, 64)
        Bn, Tq, _ = q.shape
        Tk = k.shape[1]
        residual = q
        mask = attn_mask.astype(jnp.float32)
        qh = (q @ Wq + bq).reshape(Bn, Tq, H, DK)
        kh = (k @ Wk + bk).reshape(Bn, Tk, H, DK)
        vh = (v @ Wv + bv).reshape(Bn, Tk, H, DK)
        attn = jnp.einsum('bqhd,bkhd->hbqk', qh, kh)
        attn = attn * mask[None]
        attn = attn - jnp.max(attn)
        attn = jnp.exp(attn) * mask[None]
        attn = attn / (jnp.sum(attn, axis=-1, keepdims=True) + 1e-15)
        out = jnp.einsum('hbqk,bkhd->bqhd', attn, vh).reshape(Bn, Tq, H * DK)
        out = out @ Wo + bo
        x = out + residual
        mu = jnp.mean(x, axis=-1, keepdims=True)
        var = jnp.mean((x - mu) ** 2, axis=-1, keepdims=True)
        return (x - mu) / jnp.sqrt(var + 1e-05) * gamma + beta
    x = _L0_xattn_ref(x, ctx_1024, ctx_1024, mask_BxSxS2_ik1, L0_xattn_Wq, L0_xattn_bq, L0_xattn_Wk, L0_xattn_bk, L0_xattn_Wv, L0_xattn_bv, L0_xattn_Wo, L0_xattn_bo, L0_xattn_gamma, L0_xattn_beta)
    return x

_drawn_inputs = setup_inputs


def setup_inputs(seed=0):
    import zlib

    import numpy as np

    out = dict(_drawn_inputs(seed))
    spreads = {'L0_xattn_bq': (0.0, 0.285),
     'L0_xattn_bk': (0.0, 2.0),
     'L0_xattn_bv': (0.0, 0.1),
     'L0_xattn_bo': (0.0, 0.1),
     'L0_xattn_gamma': (1.0, 0.2),
     'L0_xattn_beta': (0.0, 0.1)}
    factors = {}
    for name, (base, spread) in spreads.items():
        noise = np.random.default_rng([zlib.crc32(name.encode()), seed]).standard_normal(out[name].shape)
        drawn = base * np.exp(spread * noise) if base else spread * noise
        out[name] = jnp.asarray(drawn.astype(out[name].dtype))
    for name, factor in factors.items():
        out[name] = (out[name] * factor).astype(out[name].dtype)
    return out
```

```python
from contextlib import ExitStack

import concourse.bass as bass
from concourse import mybir

F32 = mybir.dt.float32
F16 = mybir.dt.float16
BF16 = mybir.dt.bfloat16
I32 = mybir.dt.int32
ALU = mybir.AluOpType
ACT = mybir.ActivationFunctionType
AX = mybir.AxisListType

P = 128
B, T, D = 16, 1024, 512
H, DK, NK = 16, 64, 64
HD = H * DK
HK = H * NK
DC = D // P
NP = HD // P
GB = 2
NG = B // GB
TT = 512
UB = T // TT
UNITS = GB * UB
NU = B * UB
TB = TT // P
KC = GB * NK
GT = NP * DC // 2
UT = GB * NP

W_SCALE, CTX_SCALE, X_SCALE = 64.0, 4.0, 4.0
K_SCALE, G_SCALE = 8.0, 16.0
V_SCALE, U_SCALE, P_SCALE = 32.0, 64.0, 1024.0
MASKED = -1.0e30
TINY, LN_EPS = 1e-15, 1e-5

COPIES = 3


def build(nc, xT, x, ctxT, maskT, wk, wqT, wv, wo, bk, bq, bv, bo, gamma, beta,
          sel_sum_d, sel_bc_d, part_d, out):
    scores_d = nc.dram_tensor("scores", (NU, P, NP * TT), F32, kind="Internal").ap()

    with ExitStack() as ctx:
        def sb(name, shape, dt=F32, scope=ctx):
            return scope.enter_context(nc.sbuf_tensor(name, shape, dt))

        wv_hi, wv_lo = sb("wv_hi", [P, DC, HD], F16), sb("wv_lo", [P, DC, HD], F16)
        wo_hi, wo_lo = sb("wo_hi", [P, NP, D], F16), sb("wo_lo", [P, NP, D], F16)
        bkv = sb("bkv", [P, 2, NP])
        ctx32 = sb("ctx32", [P, DC, KC])
        ctx_hi, ctx_lo = sb("ctx_hi", [P, DC, KC], F16), sb("ctx_lo", [P, DC, KC], F16)
        kv32 = sb("kv32", [P, NP, KC])
        kv_hi, kv_lo = sb("kv_hi", [P, NP, GB, 2, NK], F16), sb("kv_lo", [P, NP, GB, 2, NK], F16)
        score_max, key_max, neg_max = sb("score_max", [P, 1]), sb("key_max", [P, 1]), sb("neg_max", [P, 1])

        scores_phase(nc, xT, ctxT, maskT, wk, wqT, wv, wo, bk, bq, bv, scores_d,
                     wv_hi, wv_lo, wo_hi, wo_lo, bkv, ctx32, ctx_hi, ctx_lo, kv32, kv_hi, kv_lo,
                     score_max, key_max, neg_max)
        output_phase(nc, x, ctxT, scores_d, bo, gamma, beta, sel_sum_d, sel_bc_d, part_d, out,
                     wv_hi, wv_lo, wo_hi, wo_lo, bkv, ctx32, ctx_hi, ctx_lo, kv32, kv_hi, kv_lo, neg_max)


def split_product(pe, out, lhs, rhs, first, last):
    (lhs_hi, lhs_lo), (rhs_hi, rhs_lo) = lhs, rhs
    pe.matmul(out, lhs_hi, rhs_hi, start=first, stop=False)
    pe.matmul(out, lhs_hi, rhs_lo, start=False, stop=False)
    return pe.matmul(out, lhs_lo, rhs_hi, start=False, stop=last)


def project_heads(pe, banks, w_hi, w_lo, ctx_hi, ctx_lo, ready):
    for p in range(NP):
        o = banks[p // 4][:, (p % 4) * KC:(p % 4 + 1) * KC]
        cols = slice(p * P, (p + 1) * P)
        for c in range(DC):
            mm = split_product(pe, o, (w_hi[:, c, cols], w_lo[:, c, cols]),
                               (ctx_hi[:, c, :], ctx_lo[:, c, :]), c == 0, c == DC - 1)
        if p % 4 == 3:
            mm.then_inc(ready, 1)


def halves(hi, kv32):
    for h in range(2):
        rows = slice(h * DK, (h + 1) * DK)
        yield (hi[rows, :, :, h, :].rearrange("r p b k -> r (p b) k"),
               kv32[rows, :, :].rearrange("r p (b k) -> r (p b) k", b=GB))


def scores_phase(nc, xT, ctxT, maskT, wk, wqT, wv, wo, bk, bq, bv, scores_d,
                 wv_hi, wv_lo, wo_hi, wo_lo, bkv, ctx32, ctx_hi, ctx_lo, kv32, kv_hi, kv_lo,
                 score_max, key_max, neg_max):
    with ExitStack() as ctx:
        def sb(name, shape, dt=F32):
            return ctx.enter_context(nc.sbuf_tensor(name, shape, dt))

        def sem(name):
            return ctx.enter_context(nc.semaphore(name))

        def bank(name):
            return ctx.enter_context(nc.psum_tensor(name, [P, 512], F32))

        wk_hi, wk_lo = sb("wk_hi", [P, DC, HD], F16), sb("wk_lo", [P, DC, HD], F16)
        wq_hi, wq_lo = sb("wq_hi", [P, NP, D], F16), sb("wq_lo", [P, NP, D], F16)
        w32 = sb("w32", [P, 4, 1024])
        bq32, bq16 = sb("bq32", [P, NP]), sb("bq16", [P, NP, 2], F16)
        x32 = sb("x32", [P, 2, DC, TT])
        x_hi, x_lo = sb("x_hi", [P, 2, DC, TT], F16), sb("x_lo", [P, 2, DC, TT], F16)
        g_hi, g_lo = sb("g_hi", [P, NP, DC, GB, P], F16), sb("g_lo", [P, NP, DC, GB, P], F16)
        c_raw, c_bias = sb("c_raw", [P, NP * GB]), sb("c_bias", [P, NP * GB])
        mask32, mask_add = sb("mask32", [P, T], I32), sb("mask_add", [P, 2, T])
        s32 = sb("s32", [P, 2, NP, TT])
        unit_max, mask_min, least = sb("unit_max", [P, 1]), sb("mask_min", [P, 1]), sb("least", [P, 1])

        ps_s = [bank(f"ps_s{i}") for i in range(4)]
        ps_g = [bank(f"ps_g{i}") for i in range(2)]
        ps_k = [bank(f"ps_k{i}") for i in range(2)]

        w_in = [sem(f"w_in{i}") for i in range(4)]
        w_hi_done, w_lo_done = sem("w_hi_done"), sem("w_lo_done")
        small_in, bq_done = sem("small_in"), sem("bq_done")
        ctx_in, ctx_hi_done, ctx_lo_done = sem("ctx_in"), sem("ctx_hi_done"), sem("ctx_lo_done")
        x_in = [sem(f"x_in{i}") for i in range(2)]
        x_hi_done, x_lo_done = sem("x_hi_done"), sem("x_lo_done")
        mask_in, mask_ready = sem("mask_in"), sem("mask_ready")
        zeroed = sem("zeroed")
        k_summed, k32_done = sem("k_summed"), sem("k32_done")
        k_hi_done, k_lo_done = sem("k_hi_done"), sem("k_lo_done")
        c_summed, c_ready, c_rawed = sem("c_summed"), sem("c_ready"), sem("c_rawed")
        g_summed, g_hi_done, g_lo_done = sem("g_summed"), sem("g_hi_done"), sem("g_lo_done")
        s_summed, s_out, s_masked = sem("s_summed"), sem("s_out"), sem("s_masked")
        unit_reduced, max_steps = sem("unit_reduced"), sem("max_steps")
        s_stored = [sem(f"s_stored{i}") for i in range(2)]
        max_local, max_global, max_done = sem("max_local"), sem("max_global"), sem("max_done")

        def rows(w):
            return w.rearrange("c p n -> c p n")
        first_weights = [(wk, wk_hi, wk_lo), (wqT, wq_hi, wq_lo)]
        later_weights = [(wv, wv_hi, wv_lo), (wo, wo_hi, wo_lo)]

        def chunk(i):
            w, hi, lo = (first_weights + later_weights)[i // 4]
            c = i % 4
            flat = lambda a: a.rearrange("p c n -> p (c n)")[:, c * 1024:(c + 1) * 1024]
            return w[c], flat(hi[:, :, :]), flat(lo[:, :, :])

        block = ctx.enter_context(nc.Block())

        @block.sync
        def _(sp):
            def load_weight(i):
                if i >= 4:
                    sp.wait_ge(w_lo_done, i - 3)
                sp.dma_start(w32[:, i % 4, :], chunk(i)[0]).then_inc(w_in[i % 4], 16)

            def load_ctx(g):
                sp.dma_start(ctx32[:, :, :], ctxT[:, :, bass.ds(g * KC, KC)].rearrange("c p k -> p c k"))\
                  .then_inc(ctx_in, 16)

            def load_x(n, b, u):
                sp.wait_ge(x_lo_done, n + 1)
                sp.dma_start(x32[:, u % 2, :, :],
                             xT[bass.ds(b, 1), :, :, (u % 2) * TT:(u % 2 + 1) * TT]
                             .rearrange("a c p t -> p (a c) t")).then_inc(x_in[u % 2], 16)

            def load_mask(b):
                sp.wait_ge(mask_ready, b + 1)
                for h in range(2):
                    sp.dma_start(mask32[h * NK:(h + 1) * NK, :],
                                 maskT[bass.ds(b, 1), :, :].rearrange("a k t -> (a k) t")).then_inc(mask_in, 16)

            def store_scores(n, u):
                sp.wait_ge(s_masked, (n + 1) * NP)
                sp.dma_start(scores_d[bass.ds(n, 1), :, :].rearrange("a p n -> p (a n)"),
                             s32[:, u % 2, :, :].rearrange("r p t -> r (p t)")).then_inc(s_stored[u % 2], 16)

            for i in range(2):
                sp.sem_inc(s_stored[i], 16)
            load_ctx(0)
            for half, w in enumerate((bk, bv)):
                sp.dma_start(bkv[:, half, :], w).then_inc(small_in, 16)
            sp.dma_start(bq32[:, :], bq).then_inc(small_in, 16)
            for i in range(8):
                load_weight(i)
            load_mask(0)
            load_x(0, 0, 0)
            load_x(1, 0, 1)

            def group(g, last):
                load_mask(g * GB + 1)
                if not last:
                    sp.wait_ge(ctx_lo_done, g + 1)
                    load_ctx(g + 1)
                for u in range(UNITS):
                    if not (last and u >= UNITS - 2):
                        load_x(g * UNITS + u + 2, g * GB + (u + 2) // UB, u)
                    if u == 2 and not last:
                        load_mask(g * GB + 2)
                    if last and u < 2:
                        for i in range(8 + 4 * u, 12 + 4 * u):
                            load_weight(i)
                    store_scores(g * UNITS + u, u)

            with sp.Fori(0, NG - 1) as g:
                group(g, False)
            group(NG - 1, True)
            for i in range(2):
                sp.wait_ge(s_stored[i], 16 + 8 * NU)

        @block.tensor
        def _(pe):
            pe.sem_inc(s_summed, 2 * NP)

            def project(g):
                pe.wait_ge(ctx_lo_done, g + 1)
                pe.wait_ge(c_ready, g + 1)
                project_heads(pe, ps_k, wk_hi, wk_lo, ctx_hi, ctx_lo, k_summed)

            def bias(g):
                pe.wait_ge(k_hi_done, 2 * g + 2)
                pe.wait_ge(k_lo_done, 2 * g + 2)
                for p in range(NP):
                    for b in range(GB):
                        o = ps_k[0][:, 2 * (GB * p + b):2 * (GB * p + b) + 2]
                        for k, half in enumerate((kv_hi, kv_lo)):
                            mm = pe.matmul(o, half[:, p, b, :, :].rearrange("r h k -> r (h k)"), bq16[:, p, :],
                                           start=(k == 0), stop=(k == 1))
                mm.then_inc(c_summed, 1)

            def fold_q(g):
                for i in range(GT):
                    p, dp = i // 2, i % 2
                    pe.wait_ge(g_lo_done, g * GT + i + 1)
                    k2 = tuple(k[:, p, :, :, :].rearrange("r b h k -> r (b h k)") for k in (kv_hi, kv_lo))
                    for j in range(2):
                        cols = slice((2 * dp + j) * P, (2 * dp + j + 1) * P)
                        mm = split_product(pe, ps_g[i % 2][:, j * GB * P:(j + 1) * GB * P],
                                           (wq_hi[:, p, cols], wq_lo[:, p, cols]), k2, True, True)
                    mm.then_inc(g_summed, 1)

            def scores(g, u):
                n, b = g * UNITS + u, u // UB
                pe.wait_ge(x_lo_done, n + 3)
                for p in range(NP):
                    if u == 0:
                        pe.wait_ge(g_lo_done, g * GT + 2 * p + 4)
                    pe.wait_ge(s_out, n * NP + p + 1)
                    for c in range(DC):
                        mm = split_product(pe, ps_s[p % 4][:, :],
                                           (g_hi[:, p, c, b, :], g_lo[:, p, c, b, :]),
                                           (x_hi[:, u % 2, c, :], x_lo[:, u % 2, c, :]), c == 0, c == DC - 1)
                    mm.then_inc(s_summed, 1)

            def group(g, last):
                bias(g)
                fold_q(g)
                for u in range(UNITS):
                    scores(g, u)
                    if u == UNITS - 2 and not last:
                        project(g + 1)

            pe.wait_ge(w_lo_done, 4)
            project(0)
            pe.wait_ge(w_lo_done, 8)
            pe.wait_ge(bq_done, 2)
            with pe.Fori(0, NG - 1) as g:
                group(g, False)
            group(NG - 1, True)

        @block.scalar
        def _(act):
            act.sem_inc(s_out, 4)

            def split_weight(i):
                act.wait_ge(w_in[i % 4], 16 * (i // 4 + 1))
                act.activation(chunk(i)[1], w32[:, i % 4, :], ACT.Copy, scale=W_SCALE).then_inc(w_hi_done, 1)

            def split_ctx(g):
                act.wait_ge(ctx_in, 16 * (g + 1))
                act.activation(ctx_hi[:, :, :], ctx32[:, :, :], ACT.Copy, scale=CTX_SCALE).then_inc(ctx_hi_done, 1)

            def round_x(g, u):
                act.wait_ge(x_in[u % 2], g * (8 * UNITS) + 16 * (u // 2 + 1))
                act.wait_ge(s_summed, (g * UNITS + u + 1) * NP)
                act.activation(x_hi[:, u % 2, :, :], x32[:, u % 2, :, :], ACT.Copy, scale=X_SCALE)\
                   .then_inc(x_hi_done, 1)

            def round_k(g):
                if not (isinstance(g, int) and g == 0):
                    act.wait_ge(k_lo_done, 2 * g)
                for p in range(NP):
                    if p % 4 == 0:
                        act.wait_ge(k_summed, 2 * g + p // 4 + 1)
                    act.activation(kv32[:, p, :], ps_k[p // 4][:, (p % 4) * KC:(p % 4 + 1) * KC], ACT.Identity,
                                   bias=bkv[:, 0, p:p + 1], scale=1 / (W_SCALE * CTX_SCALE)).then_inc(k32_done, 1)
                act.wait_ge(k32_done, NP * (g + 1))
                for o, i in halves(kv_hi, kv32):
                    act.activation(o, i, ACT.Copy, scale=K_SCALE).then_inc(k_hi_done, 1)

            def round_g(g):
                act.wait_ge(s_summed, (g * UNITS + 2) * NP)
                for i in range(GT):
                    p, dp = i // 2, i % 2
                    act.wait_ge(g_summed, g * GT + i + 1)
                    act.activation(g_hi[:, p, 2 * dp:2 * dp + 2, :, :].rearrange("r c b k -> r (c b k)"),
                                   ps_g[i % 2][:, :], ACT.Copy, scale=G_SCALE / (W_SCALE * K_SCALE))\
                       .then_inc(g_hi_done, 1)

            def scores_out(g, u):
                n = g * UNITS + u
                act.wait_ge(s_stored[u % 2], g * (8 * UNITS) + 16 * (u // 2 + 1))
                act.wait_ge(unit_reduced, n + 1)
                if u == 0:
                    act.wait_ge(c_ready, g + 2)
                for p in range(NP):
                    act.wait_ge(s_summed, n * NP + p + 1 + 2 * NP)
                    k = GB * p + u // UB
                    act.activation(s32[:, u % 2, p, :], ps_s[p % 4][:, :], ACT.Identity, bias=c_bias[:, k:k + 1],
                                   scale=1 / (G_SCALE * X_SCALE)).then_inc(s_out, 1)

            def group(g, last):
                round_g(g)
                for u in range(UNITS):
                    if not (last and u == UNITS - 1):
                        round_x(g, u + 1)
                    scores_out(g, u)
                    if u == 1 and not last:
                        act.wait_ge(k_summed, 2 * g + 2)
                        split_ctx(g + 1)
                    if u == UNITS - 2 and not last:
                        act.wait_ge(g_summed, (g + 1) * GT)
                        round_k(g + 1)
                    if last and u < 2:
                        for i in range(8 + 4 * u, 12 + 4 * u):
                            split_weight(i)

            split_ctx(0)
            act.wait_ge(small_in, 48)
            act.activation(bq16[:, :, 0], bq32[:, :], ACT.Copy, scale=W_SCALE).then_inc(bq_done, 1)
            for i in range(8):
                split_weight(i)
                if i == 3:
                    act.wait_ge(zeroed, 2)
            round_k(0)
            round_x(0, 0)
            with act.Fori(0, NG - 1) as g:
                group(g, False)
            group(NG - 1, True)

        @block.vector
        def _(dve):
            dve.sem_inc(x_lo_done, 2)
            dve.sem_inc(mask_ready, 1)
            dve.sem_inc(g_lo_done, 2)
            dve.sem_inc(unit_reduced, 2)
            dve.sem_inc(c_ready, 1)
            dve.memset(kv_hi[:, :, :, :, :], 0.0).then_inc(zeroed, 1)
            dve.memset(kv_lo[:, :, :, :, :], 0.0).then_inc(zeroed, 1)
            dve.memset(score_max[:, :], MASKED).then_inc(max_steps, 1)
            dve.memset(least[:, :], 0.0).then_inc(max_steps, 1)
            dve.wait_ge(max_steps, 2)

            def split_weight(i):
                dve.wait_ge(w_hi_done, i + 1)
                _, hi, lo = chunk(i)
                dve.scalar_tensor_tensor(lo, w32[:, i % 4, :], W_SCALE, hi, ALU.mult, ALU.subtract)\
                   .then_inc(w_lo_done, 1)

            def split_ctx(g):
                dve.wait_ge(ctx_hi_done, g + 1)
                dve.scalar_tensor_tensor(ctx_lo[:, :, :], ctx32[:, :, :], CTX_SCALE, ctx_hi[:, :, :],
                                         ALU.mult, ALU.subtract).then_inc(ctx_lo_done, 1)

            def split_x(g, u):
                dve.wait_ge(x_hi_done, g * UNITS + u + 1)
                dve.scalar_tensor_tensor(x_lo[:, u % 2, :, :], x32[:, u % 2, :, :], X_SCALE, x_hi[:, u % 2, :, :],
                                         ALU.mult, ALU.subtract).then_inc(x_lo_done, 1)

            def split_k(g):
                dve.wait_ge(k_hi_done, 2 * g + 2)
                for (o, i), (hi, _) in zip(halves(kv_lo, kv32), halves(kv_hi, kv32)):
                    dve.scalar_tensor_tensor(o, i, K_SCALE, hi, ALU.mult, ALU.subtract).then_inc(k_lo_done, 1)

            def split_g(g):
                for i in range(GT):
                    p, dp = i // 2, i % 2
                    at = lambda a: a[:, p, 2 * dp:2 * dp + 2, :, :].rearrange("r c b k -> r (c b k)")
                    dve.wait_ge(g_hi_done, g * GT + i + 1)
                    dve.scalar_tensor_tensor(at(g_lo), ps_g[i % 2][:, :], G_SCALE / (W_SCALE * K_SCALE), at(g_hi),
                                             ALU.mult, ALU.subtract).then_inc(g_lo_done, 1)

            def bias(g):
                dve.wait_ge(c_summed, g + 1)
                dve.tensor_reduce(c_raw[:, :], ps_k[0][:, 0:2 * NP * GB].rearrange("r (n k) -> r n k", k=2),
                                  axis=AX.X, op=ALU.add).then_inc(c_rawed, 1)
                dve.wait_ge(c_rawed, g + 1)
                dve.wait_ge(s_out, g * UNITS * NP + 4)
                dve.tensor_scalar(c_bias[:, :], c_raw[:, :], 1 / (W_SCALE * K_SCALE), None, ALU.mult)\
                   .then_inc(c_ready, 1)

            STEPS = 2 * GB + UNITS

            def mask(g, j, step):
                b = g * GB + j
                dve.wait_ge(mask_in, 32 * (b + 1))
                if j == 0:
                    dve.wait_ge(unit_reduced, g * UNITS + 2)
                dve.tensor_scalar(mask_add[:, j, :], mask32[:, :], -MASKED, MASKED, ALU.mult, ALU.add)\
                   .then_inc(mask_ready, 1)
                dve.wait_ge(mask_ready, b + 2)
                dve.tensor_reduce(mask_min[:, :], mask_add[:, j, :], axis=AX.X, op=ALU.min).then_inc(max_steps, 1)
                dve.wait_ge(max_steps, g * STEPS + 2 + step + 1)
                dve.tensor_tensor(least[:, :], least[:, :], mask_min[:, :], ALU.min).then_inc(max_steps, 1)
                dve.wait_ge(max_steps, g * STEPS + 2 + step + 2)
                return step + 2

            def mask_scores(g, u, step):
                n, j, t0 = g * UNITS + u, u // UB, (u % UB) * TT
                for p in range(NP):
                    dve.wait_ge(s_out, n * NP + p + 1 + 4)
                    dve.tensor_tensor(s32[:, u % 2, p, :], s32[:, u % 2, p, :], mask_add[:, j, t0:t0 + TT],
                                      ALU.add).then_inc(s_masked, 1)
                dve.wait_ge(s_masked, (n + 1) * NP)
                dve.tensor_reduce(unit_max[:, :], s32[:, u % 2, :, :].rearrange("r p t -> r (p t)"),
                                  axis=AX.X, op=ALU.max).then_inc(unit_reduced, 1)
                dve.wait_ge(unit_reduced, n + 3)
                dve.tensor_tensor(score_max[:, :], score_max[:, :], unit_max[:, :], ALU.max).then_inc(max_steps, 1)
                dve.wait_ge(max_steps, g * STEPS + 2 + step + 1)
                return step + 1

            def group(g, last):
                step = 0
                bias(g)
                split_g(g)
                for u in range(UNITS):
                    if not (last and u == UNITS - 1):
                        split_x(g, u + 1)
                    if u % UB == 0:
                        step = mask(g, u // UB, step)
                    step = mask_scores(g, u, step)
                    if u == 1 and not last:
                        split_ctx(g + 1)
                    if u == UNITS - 2 and not last:
                        split_k(g + 1)
                    if last and u < 2:
                        for i in range(8 + 4 * u, 12 + 4 * u):
                            split_weight(i)
                assert step == STEPS

            split_ctx(0)
            dve.wait_ge(bq_done, 1)
            dve.scalar_tensor_tensor(bq16[:, :, 1], bq32[:, :], W_SCALE, bq16[:, :, 0], ALU.mult, ALU.subtract)\
               .then_inc(bq_done, 1)
            for i in range(8):
                split_weight(i)
            split_k(0)
            split_x(0, 0)
            with dve.Fori(0, NG - 1) as g:
                group(g, False)
            group(NG - 1, True)

            dve.tensor_scalar(key_max[:, :], least[:, :], -1.0, MASKED, ALU.mult, ALU.add).then_inc(max_steps, 1)
            dve.wait_ge(max_steps, NG * STEPS + 3)
            dve.tensor_tensor(score_max[:, :], score_max[:, :], key_max[:, :], ALU.max).then_inc(max_local, 1)
            dve.wait_ge(max_global, 1)
            dve.tensor_scalar(neg_max[:, :], key_max[:, :], -1.0, None, ALU.mult).then_inc(max_done, 1)

        @block.gpsimd
        def _(pool):
            pool.wait_ge(max_local, 1)
            pool.partition_all_reduce(key_max[:, :], score_max[:, :], P, bass.bass_isa.ReduceOp.max)\
                .then_inc(max_global, 1)


def output_phase(nc, x, ctxT, scores_d, bo, gamma, beta, sel_sum_d, sel_bc_d, part_d, out,
                 wv_hi, wv_lo, wo_hi, wo_lo, bkv, ctx32, ctx_hi, ctx_lo, kv32, kv_hi, kv_lo, neg_max):
    with ExitStack() as ctx:
        def sb(name, shape, dt=F32):
            return ctx.enter_context(nc.sbuf_tensor(name, shape, dt))

        def sem(name):
            return ctx.enter_context(nc.semaphore(name))

        def bank(name):
            return ctx.enter_context(nc.psum_tensor(name, [P, 512], F32))

        u_hi, u_lo = sb("u_hi", [P, GB, NP, D], F16), sb("u_lo", [P, GB, NP, D], F16)
        e32 = sb("e32", [P, 2, NP, TT])
        p_hi, p_lo = sb("p_hi", [P, 2, NP, TT], F16), sb("p_lo", [P, 2, NP, TT], F16)
        y32 = sb("y32", [P, UNITS, TB, D])
        gamma_b, beta_b, bo_b = sb("gamma_b", [P, D]), sb("beta_b", [P, D]), sb("bo_b", [P, D])
        sel_sum, sel_bc32 = sb("sel_sum", [P, 2, 32]), y32[:, 0, 0:2, :].rearrange("p t (n k) -> p (t n) k", k=P)
        sel_bc, part = sb("sel_bc", [P, NP, P], BF16), sb("part", [P, 2])
        den, r32, rest = sb("den", [P, TT]), sb("r32", [P, TT]), sb("rest", [P, TT])
        r_hi, r_mid, r_all = sb("r_hi", [P, TT], BF16), sb("r_mid", [P, TT], BF16), sb("r_all", [P, TT], BF16)
        stats, mean_var = sb("stats", [P, TB, 6]), sb("mean_var", [P, TB, 2])
        var_eps, rstd, minus_half = sb("var_eps", [P, TB]), sb("rstd", [P, TB]), sb("minus_half", [P, 1])
        ln_eps = sb("ln_eps", [P, 1])

        ps_sum = bank("ps_sum")
        ps_bc = [bank(f"ps_bc{i}") for i in range(2)]
        ps_o = [bank(f"ps_o{i}") for i in range(2)]
        ps_u = [bank(f"ps_u{i}") for i in range(2)]

        small_in, sel_done, consts_done = sem("small2_in"), sem("sel_done"), sem("consts_done")
        ctx_in, ctx_hi_done, ctx_lo_done = sem("ctx2_in"), sem("ctx2_hi_done"), sem("ctx2_lo_done")
        e_in = [sem(f"e_in{i}") for i in range(2)]
        x_in = [sem(f"xres_in{i}") for i in range(UNITS)]
        v_summed, v32_done = sem("v_summed"), sem("v32_done")
        v_hi_done, v_lo_done = sem("v_hi_done"), sem("v_lo_done")
        u_summed, u_hi_done, u_lo_done = sem("u_summed"), sem("u_hi_done"), sem("u_lo_done")
        exp_done, e_summed = sem("exp_done"), sem("e_summed")
        den_done, r_done, r_hi_done = sem("den_done"), sem("r_done"), sem("r_hi_done")
        rest_done, r_mid_done, r_all_done = sem("rest_done"), sem("r_mid_done"), sem("r_all_done")
        r_spread, p_scaled = sem("r_spread"), sem("p_scaled")
        p_hi_done, p_lo_done = sem("p_hi_done"), sem("p_lo_done")
        o_summed, y_added, mean_done = sem("o_summed"), sem("y_added"), sem("mean_done")
        eps_added, rstd_done = sem("eps_added"), sem("rstd_done")
        normed, scaled, shifted, bo_added = sem("normed"), sem("scaled"), sem("shifted"), sem("bo_added")
        y_stored = [sem(f"y_stored{i}") for i in range(UNITS)]

        def tokens(a, b, u):
            t0 = (u % UB) * TT
            return a[bass.ds(b, 1), t0:t0 + TT, :].rearrange("a (n p) d -> p (a n) d", p=P)

        block = ctx.enter_context(nc.Block())

        @block.sync
        def _(sp):
            def load_scores(n, u):
                sp.wait_ge(p_lo_done, 4 * n + 4)
                sp.dma_start(e32[:, u % 2, :, :].rearrange("r p t -> r (p t)"),
                             scores_d[bass.ds(n, 1), :, :].rearrange("a p n -> p (a n)")).then_inc(e_in[u % 2], 16)

            def load_x(g, u):
                s = u % UNITS
                sp.wait_ge(y_stored[s], 16 * g + 16 * (u // UNITS) + 16)
                sp.dma_start(y32[:, s, :, :], tokens(x, g * GB + u // UB, u)).then_inc(x_in[s], 16)

            def load_ctx(g):
                sp.dma_start(ctx32[:, :, :], ctxT[:, :, bass.ds(g * KC, KC)].rearrange("c p k -> p c k"))\
                  .then_inc(ctx_in, 16)

            def store_y(g, u):
                sp.wait_ge(shifted, (g * UNITS + u + 1) * TB)
                sp.dma_start(tokens(out, g * GB + u // UB, u), y32[:, u, :, :]).then_inc(y_stored[u], 16)

            for i in range(UNITS):
                sp.sem_inc(y_stored[i], 16)
            load_ctx(0)
            sp.dma_start(sel_sum[:, :, :], sel_sum_d).then_inc(small_in, 16)
            sp.dma_start(sel_bc32, sel_bc_d).then_inc(small_in, 16)
            sp.dma_start(part[:, :], part_d).then_inc(small_in, 16)
            load_scores(0, 0)
            load_scores(1, 1)
            for to, of in ((gamma_b, gamma), (beta_b, beta), (bo_b, bo)):
                sp.dma_start(to[:, :], of.rearrange("(a d) -> a d", a=1).to_broadcast([P, D])).then_inc(small_in, 16)
            sp.wait_ge(sel_done, 1)
            load_x(0, 0)
            load_x(0, 1)

            def group(g, last):
                if not last:
                    sp.wait_ge(ctx_lo_done, g + 1)
                    load_ctx(g + 1)
                for u in range(UNITS):
                    if not (last and u >= UNITS - 2):
                        load_scores(g * UNITS + u + 2, u)
                        load_x(g, u + 2)
                    store_y(g, u)

            with sp.Fori(0, NG - 1) as g:
                group(g, False)
            group(NG - 1, True)
            for i in range(UNITS):
                sp.wait_ge(y_stored[i], 16 + 16 * NG)

        @block.tensor
        def _(pe):
            pe.sem_inc(o_summed, 2 * TB)

            def project(g):
                pe.wait_ge(ctx_lo_done, g + 1)
                pe.wait_ge(u_lo_done, g * UT + 2)
                project_heads(pe, ps_u, wv_hi, wv_lo, ctx_hi, ctx_lo, v_summed)

            def fold_o(g):
                pe.wait_ge(v_hi_done, 2 * g + 2)
                pe.wait_ge(v_lo_done, 2 * g + 2)
                for i in range(UT):
                    b, p = i // NP, i % NP
                    pe.wait_ge(u_lo_done, g * UT + i + 1)
                    v2 = tuple(v[:, p, b, :, :].rearrange("r h k -> r (h k)") for v in (kv_hi, kv_lo))
                    split_product(pe, ps_u[i % 2][:, :], v2, (wo_hi[:, p, :], wo_lo[:, p, :]), True, True)\
                        .then_inc(u_summed, 1)

            def sums(n, s):
                pe.wait_ge(exp_done, 2 * n + 2)
                pe.wait_ge(den_done, n + 1)
                for r in range(2):
                    for q in range(4):
                        mm = pe.matmul(ps_sum[32 * q:32 * q + 32, :], sel_sum[:, r, :], e32[:, s, 4 * r + q, :],
                                       start=(r == 0), stop=(r == 1), skip_group_check=True)
                mm.then_inc(e_summed, 1)

            def spread(n, p):
                if p == 0:
                    pe.wait_ge(r_all_done, n + 1)
                pe.wait_ge(p_scaled, n * NP + p + 1)
                pe.matmul(ps_bc[p % 2][:, :], sel_bc[:, p, :], r_all[:, :], start=True, stop=True)\
                  .then_inc(r_spread, 1)

            def unit(g, u, last):
                n, s, b = g * UNITS + u, u % 2, u // UB
                more = not (last and u == UNITS - 1)
                if more:
                    sums(n + 1, (u + 1) % 2)
                slots = {(1, 0): 0, (1, 3): 1, (1, 5): 2, (2, 0): 3, (2, 3): 4, (2, 5): 5, (3, 0): 6, (3, 3): 7}
                for t in range(TB):
                    pe.wait_ge(y_added, n * TB + t + 1)
                    for p in range(NP):
                        if more and (t, p) in slots:
                            spread(n + 1, slots[t, p])
                        if t == 0 and p % 2 == 0:
                            pe.wait_ge(p_lo_done, 4 * n + p // 2 + 1 + 8)
                        if t == 0 and u % UB == 0:
                            pe.wait_ge(u_lo_done, g * UT + b * NP + p + 1 + 2)
                        cols = slice(t * P, (t + 1) * P)
                        mm = split_product(pe, ps_o[t % 2][:, :], (p_hi[:, s, p, cols], p_lo[:, s, p, cols]),
                                           (u_hi[:, b, p, :], u_lo[:, b, p, :]), p == 0, p == NP - 1)
                    mm.then_inc(o_summed, 1)

            def group(g, last):
                fold_o(g)
                for u in range(UNITS):
                    unit(g, u, last)
                    if u == UNITS - 2 and not last:
                        project(g + 1)

            project(0)
            pe.wait_ge(small_in, 16 * 6)
            sums(0, 0)
            pe.wait_ge(sel_done, 1)
            for p in range(NP):
                spread(0, p)
            with pe.Fori(0, NG - 1) as g:
                group(g, False)
            group(NG - 1, True)

        @block.scalar
        def _(act):
            def exps(n, u, half):
                act.wait_ge(e_in[u % 2], 8 * n + 16 - 8 * (u % 2))
                e = e32[:, u % 2, 4 * half:4 * half + 4, :]
                act.activation(e, e, ACT.Exp, bias=neg_max[:, 0:1]).then_inc(exp_done, 1)

            def round_ctx(g):
                act.wait_ge(ctx_in, 16 * (g + 1))
                act.activation(ctx_hi[:, :, :], ctx32[:, :, :], ACT.Copy, scale=CTX_SCALE).then_inc(ctx_hi_done, 1)

            def round_v(g):
                if not (isinstance(g, int) and g == 0):
                    act.wait_ge(v_lo_done, 2 * g)
                for p in range(NP):
                    if p % 4 == 0:
                        act.wait_ge(v_summed, 2 * g + p // 4 + 1)
                    act.activation(kv32[:, p, :], ps_u[p // 4][:, (p % 4) * KC:(p % 4 + 1) * KC], ACT.Identity,
                                   bias=bkv[:, 1, p:p + 1], scale=1 / (W_SCALE * CTX_SCALE)).then_inc(v32_done, 1)
                act.wait_ge(v32_done, NP * (g + 1))
                for o, i in halves(kv_hi, kv32):
                    act.activation(o, i, ACT.Copy, scale=V_SCALE).then_inc(v_hi_done, 1)

            def round_u(g):
                act.wait_ge(o_summed, g * (UNITS * TB) + 2 * TB)
                for i in range(UT):
                    act.wait_ge(u_summed, g * UT + i + 1)
                    act.activation(u_hi[:, i // NP, i % NP, :], ps_u[i % 2][:, :], ACT.Copy,
                                   scale=U_SCALE / (W_SCALE * V_SCALE)).then_inc(u_hi_done, 1)

            def round_r(n):
                act.wait_ge(r_done, n + 1)
                act.activation(r_hi[:, :], r32[:, :], ACT.Copy).then_inc(r_hi_done, 1)
                act.wait_ge(rest_done, n + 1)
                act.activation(r_mid[:, :], rest[:, :], ACT.Copy).then_inc(r_mid_done, 1)

            def round_p(n, s, k):
                if k == 0:
                    act.wait_ge(o_summed, TB * n + TB)
                act.wait_ge(p_scaled, n * NP + 2 * k + 2 + 2)
                act.activation(p_hi[:, s, 2 * k:2 * k + 2, :], e32[:, s, 2 * k:2 * k + 2, :], ACT.Copy)\
                   .then_inc(p_hi_done, 1)

            def group(g, last):
                round_u(g)
                for u in range(UNITS):
                    n, s = g * UNITS + u, (u + 1) % 2
                    more, more2 = not (last and u == UNITS - 1), not (last and u >= UNITS - 2)
                    if more:
                        round_r(n + 1)
                        round_p(n + 1, s, 0)
                        round_p(n + 1, s, 1)
                    if more2:
                        exps(n + 2, u, 0)
                    if more:
                        round_p(n + 1, s, 2)
                    if more2:
                        exps(n + 2, u, 1)
                    if more:
                        round_p(n + 1, s, 3)
                    if u == 1 and not last:
                        act.wait_ge(v_summed, 2 * g + 2)
                        round_ctx(g + 1)
                    if u == UNITS - 2 and not last:
                        act.wait_ge(u_summed, (g + 1) * UT)
                        round_v(g + 1)

            round_ctx(0)
            exps(0, 0, 0)
            exps(0, 0, 1)
            round_v(0)
            exps(1, 1, 0)
            exps(1, 1, 1)
            round_r(0)
            for k in range(4):
                round_p(0, 0, k)
            with act.Fori(0, NG - 1) as g:
                group(g, False)
            group(NG - 1, True)

        @block.vector
        def _(dve):
            dve.sem_inc(u_lo_done, 2)
            dve.sem_inc(den_done, 1)
            dve.sem_inc(p_scaled, 2)
            dve.sem_inc(p_lo_done, 8)
            dve.sem_inc(y_added, 2)

            def split_ctx(g):
                dve.wait_ge(ctx_hi_done, g + 1)
                dve.scalar_tensor_tensor(ctx_lo[:, :, :], ctx32[:, :, :], CTX_SCALE, ctx_hi[:, :, :],
                                         ALU.mult, ALU.subtract).then_inc(ctx_lo_done, 1)

            def split_v(g):
                dve.wait_ge(v_hi_done, 2 * g + 2)
                for (o, i), (hi, _) in zip(halves(kv_lo, kv32), halves(kv_hi, kv32)):
                    dve.scalar_tensor_tensor(o, i, V_SCALE, hi, ALU.mult, ALU.subtract).then_inc(v_lo_done, 1)

            def split_u(g):
                for i in range(UT):
                    dve.wait_ge(u_hi_done, g * UT + i + 1)
                    dve.scalar_tensor_tensor(u_lo[:, i // NP, i % NP, :], ps_u[i % 2][:, :],
                                             U_SCALE / (W_SCALE * V_SCALE), u_hi[:, i // NP, i % NP, :],
                                             ALU.mult, ALU.subtract).then_inc(u_lo_done, 1)

            def invert(n):
                dve.wait_ge(e_summed, n + 1)
                dve.tensor_scalar(den[:, :], ps_sum[:, :], TINY, None, ALU.add).then_inc(den_done, 1)
                dve.wait_ge(den_done, n + 2)
                dve.reciprocal(r32[:, :], den[:, :]).then_inc(r_done, 1)
                dve.wait_ge(r_hi_done, n + 1)
                dve.scalar_tensor_tensor(rest[:, :], r_hi[:, :], part[:, 0:1], r32[:, :], ALU.mult, ALU.add)\
                   .then_inc(rest_done, 1)
                dve.wait_ge(r_mid_done, n + 1)
                if not (isinstance(n, int) and n == 0):
                    dve.wait_ge(r_spread, n * NP)
                dve.scalar_tensor_tensor(r_all[:, :], r_mid[:, :], part[:, 1:2], rest[:, :], ALU.mult, ALU.add)\
                   .then_inc(r_all_done, 1)

            def scale_p(n, s, p):
                dve.wait_ge(r_spread, n * NP + p + 1)
                e = e32[:, s, p, :]
                dve.tensor_tensor(e, e, ps_bc[p % 2][:, :], ALU.mult).then_inc(p_scaled, 1)

            def split_p(n, s, k):
                dve.wait_ge(p_hi_done, 4 * n + k + 1)
                at = lambda a: a[:, s, 2 * k:2 * k + 2, :].rearrange("r p t -> r (p t)")
                dve.tensor_tensor(at(p_lo), at(e32), at(p_hi), ALU.subtract).then_inc(p_lo_done, 1)

            def residual(g, u, t):
                n = g * UNITS + u
                k = n * TB + t
                if t == 0:
                    dve.wait_ge(bo_added, n + 1)
                dve.wait_ge(o_summed, k + 1 + 2 * TB)
                y = y32[:, u, t, :]
                dve.scalar_tensor_tensor(y, ps_o[t % 2][:, :], 1 / (P_SCALE * U_SCALE), y, ALU.mult, ALU.add)\
                   .then_inc(y_added, 1)
                dve.wait_ge(y_added, k + 3)
                dve.bn_stats(stats[:, t, :], y)
                dve.drain()
                dve.bn_aggr(mean_var[:, t, :], stats[:, t, :]).then_inc(mean_done, 1)

            def norm(g, u, t):
                dve.wait_ge(rstd_done, (g * UNITS + u) * TB + t + 1)
                y = y32[:, u, t, :]
                dve.tensor_scalar(y, y, mean_var[:, t, 0:1], rstd[:, t:t + 1], ALU.subtract, ALU.mult)\
                   .then_inc(normed, 1)

            def group(g, last):
                split_u(g)
                for u in range(UNITS):
                    n, s = g * UNITS + u + 1, (u + 1) % 2
                    more = not (last and u == UNITS - 1)
                    scale = lambda *ps: [scale_p(n, s, p) for p in ps] if more else None
                    split = lambda *ks: [split_p(n, s, k) for k in ks] if more else None
                    if more:
                        invert(n)
                    residual(g, u, 0)
                    scale(0, 1, 2)
                    split(0)
                    residual(g, u, 1)
                    norm(g, u, 0)
                    scale(3, 4)
                    split(1)
                    scale(5)
                    residual(g, u, 2)
                    norm(g, u, 1)
                    scale(6, 7)
                    split(2, 3)
                    residual(g, u, 3)
                    norm(g, u, 2)
                    norm(g, u, 3)
                    if u == 1 and not last:
                        split_ctx(g + 1)
                    if u == UNITS - 2 and not last:
                        split_v(g + 1)

            split_ctx(0)
            dve.wait_ge(small_in, 16 * 6)
            dve.tensor_copy(sel_bc[:, :, :], sel_bc32).then_inc(sel_done, 1)
            split_v(0)
            invert(0)
            for k in range(4):
                scale_p(0, 0, 2 * k)
                scale_p(0, 0, 2 * k + 1)
                split_p(0, 0, k)
            with dve.Fori(0, NG - 1) as g:
                group(g, False)
            group(NG - 1, True)

        @block.gpsimd
        def _(pool):
            pool.memset(minus_half[:, :], -0.5).then_inc(consts_done, 1)
            pool.memset(ln_eps[:, :], LN_EPS).then_inc(consts_done, 1)
            pool.wait_ge(consts_done, 2)
            pool.wait_ge(small_in, 16 * 6)

            def add_bo(g, u):
                s = u % UNITS
                pool.wait_ge(x_in[s], 16 * g + 16 * (u // UNITS) + 16)
                for t in range(TB):
                    y = y32[:, s, t, :]
                    add = pool.tensor_tensor(y, y, bo_b[:, :], ALU.add)
                add.then_inc(bo_added, 1)

            def inv_std(g, u, t):
                k = (g * UNITS + u) * TB + t + 1
                pool.wait_ge(mean_done, k)
                pool.tensor_tensor(var_eps[:, t:t + 1], mean_var[:, t, 1:2], ln_eps[:, :], ALU.add)\
                    .then_inc(eps_added, 1)
                pool.wait_ge(eps_added, k)
                pool.tensor_tensor(rstd[:, t:t + 1], var_eps[:, t:t + 1], minus_half[:, :], ALU.pow)\
                    .then_inc(rstd_done, 1)

            def affine(g, u, t):
                k = (g * UNITS + u) * TB + t + 1
                y = y32[:, u, t, :]
                pool.wait_ge(normed, k)
                pool.tensor_tensor(y, y, gamma_b[:, :], ALU.mult).then_inc(scaled, 1)
                pool.wait_ge(scaled, k)
                pool.tensor_tensor(y, y, beta_b[:, :], ALU.add).then_inc(shifted, 1)

            def group(g, last):
                for u in range(UNITS):
                    if not (last and u == UNITS - 1):
                        add_bo(g, u + 1)
                    inv_std(g, u, 0)
                    for t in range(1, TB):
                        inv_std(g, u, t)
                        affine(g, u, t - 1)
                    affine(g, u, TB - 1)

            add_bo(0, 0)
            with pool.Fori(0, NG - 1) as g:
                group(g, False)
            group(NG - 1, True)


def kernel(**inputs):
    import numpy as np
    import concourse.bacc as bacc
    from concourse.bass_utils import run_bass_kernel_spmd

    a = {k.removeprefix("L0_xattn_"): np.asarray(v) for k, v in inputs.items()}

    def columns(v):
        return v.reshape(-1, P).T

    sel_sum = np.zeros((P, 2, 32), np.float32)
    sel_bc = np.zeros((P, NP, P), np.float32)
    part = np.zeros((P, 2), np.float32)
    for k in range(COPIES):
        for h in range(2):
            for p in range(NP):
                row = 4 * k + 2 * (p // 4) + h
                sel_sum[h * NK:(h + 1) * NK, p // 4, row] = 1.0
                sel_bc[32 * (p % 4) + row, p, h * NK:(h + 1) * NK] = P_SCALE
                part[32 * (p % 4) + row] = (-1.0 if k >= 1 else 0.0, -1.0 if k >= 2 else 0.0)

    arrays = {
        "xT": a["x"].transpose(0, 2, 1).reshape(B, DC, P, T),
        "x": a["x"],
        "ctxT": a["ctx_1024"].reshape(B * NK, D).T.reshape(DC, P, B * NK),
        "maskT": a["mask_BxSxS2_ik1"].transpose(0, 2, 1),
        "wk": a["Wk"].reshape(DC, P, HD),
        "wqT": a["Wq"].T.reshape(4, 2, P, D).transpose(0, 2, 1, 3).reshape(4, P, 2 * D),
        "wv": a["Wv"].reshape(DC, P, HD),
        "wo": a["Wo"].reshape(4, 2, P, D).transpose(0, 2, 1, 3).reshape(4, P, 2 * D),
        "bk": columns(a["bk"]), "bq": columns(a["bq"]), "bv": columns(a["bv"]),
        "bo": a["bo"], "gamma": a["gamma"], "beta": a["beta"],
        "sel_sum": sel_sum, "sel_bc": sel_bc, "part": part,
    }
    nc = bacc.Bacc("TRN2", target_bir_lowering=False, num_devices=1)
    aps = {}
    for name, v in arrays.items():
        arrays[name] = v = np.ascontiguousarray(v)
        aps[name] = nc.dram_tensor(name + "_in", v.shape, mybir.dt.from_np(v.dtype), kind="ExternalInput").ap()
    out = nc.dram_tensor("out", (B, T, D), F32, kind="ExternalOutput").ap()
    build(nc, *(aps[k] for k in ("xT", "x", "ctxT", "maskT", "wk", "wqT", "wv", "wo", "bk", "bq", "bv",
                                 "bo", "gamma", "beta", "sel_sum", "sel_bc", "part")), out)
    r = run_bass_kernel_spmd(nc, [{name + "_in": v for name, v in arrays.items()}], core_ids=[0])
    return r.results[0]["out"]
```

```python
from contextlib import ExitStack

import concourse.bass as bass
from concourse import mybir

F32 = mybir.dt.float32
F16 = mybir.dt.float16
BF16 = mybir.dt.bfloat16
I32 = mybir.dt.int32
ALU = mybir.AluOpType
ACT = mybir.ActivationFunctionType
AX = mybir.AxisListType

P = 128
B, T, D = 16, 1024, 512
H, DK, NK = 16, 64, 64
HD = H * DK
HK = H * NK
DC = D // P
NP = HD // P
GB = 2
NG = B // GB
TT = 512
UB = T // TT
UNITS = GB * UB
NU = B * UB
TB = TT // P
KC = GB * NK
GT = NP * DC // 2
SBANKS, GBANKS = 2, 4

W_SCALE, CTX_SCALE, X_SCALE = 64.0, 4.0, 4.0
K_SCALE, G_SCALE = 8.0, 16.0
V_SCALE, U_SCALE, P_SCALE = 32.0, 64.0, 1024.0
MASKED = -1.0e30
TINY, LN_EPS = 1e-15, 1e-5

COPIES = 3


def build(nc, xT, x, ctxT, ctxT_turned, maskT, wk, wqT, wv, wo, bk, bq, bv, bo, gamma, beta,
          sel_sum_d, sel_bc_d, part_d, out):
    scores_d = nc.dram_tensor("scores", (NU - UB, P, NP * TT), F32, kind="Internal").ap()

    with ExitStack() as ctx:
        def sb(name, shape, dt=F32, scope=ctx):
            return scope.enter_context(nc.sbuf_tensor(name, shape, dt))

        wv_hi, wv_lo = sb("wv_hi", [P, DC, HD], F16), sb("wv_lo", [P, DC, HD], F16)
        wo_hi, wo_lo = sb("wo_hi", [P, NP, D], F16), sb("wo_lo", [P, NP, D], F16)
        bkv = sb("bkv", [P, 2, NP])
        ctx32 = sb("ctx32", [P, DC, KC])
        ctx_hi, ctx_lo = sb("ctx_hi", [P, DC, KC], F16), sb("ctx_lo", [P, DC, KC], F16)
        kv32 = sb("kv32", [P, NP, KC])
        kv_hi, kv_lo = sb("kv_hi", [P, NP, GB, 2, NK], F16), sb("kv_lo", [P, NP, GB, 2, NK], F16)
        s32 = sb("s32", [P, 2, NP, TT])
        sel_sum, sel_bc = sb("sel_sum", [P, NP // 2, 32]), sb("sel_bc", [P, NP, 2, P], BF16)
        least = sb("least", [P, 1])
        score_max, key_max, neg_max = sb("score_max", [P, 1]), sb("key_max", [P, 1]), sb("neg_max", [P, 1])

        scores_phase(nc, xT, ctxT_turned, maskT, wk, wqT, wv, wo, bk, bq, bv, sel_bc_d, scores_d,
                     wv_hi, wv_lo, wo_hi, wo_lo, bkv, ctx32, ctx_hi, ctx_lo, kv32, kv_hi, kv_lo,
                     s32, sel_bc, score_max, least)
        output_phase(nc, x, ctxT, scores_d, bo, gamma, beta, sel_sum_d, part_d, out,
                     wv_hi, wv_lo, wo_hi, wo_lo, bkv, ctx32, ctx_hi, ctx_lo, kv32, kv_hi, kv_lo,
                     s32, sel_sum, sel_bc, score_max, least, key_max, neg_max)


def split_product(pe, out, lhs, rhs, first, last):
    (lhs_hi, lhs_lo), (rhs_hi, rhs_lo) = lhs, rhs
    pe.matmul(out, lhs_hi, rhs_hi, start=first, stop=False)
    pe.matmul(out, lhs_hi, rhs_lo, start=False, stop=False)
    return pe.matmul(out, lhs_lo, rhs_hi, start=False, stop=last)


def project_heads(pe, banks, w_hi, w_lo, ctx_hi, ctx_lo, ready, pairs=range(NP)):
    for p in pairs:
        o = banks[p // 4][:, (p % 4) * KC:(p % 4 + 1) * KC]
        cols = slice(p * P, (p + 1) * P)
        for c in range(DC):
            mm = split_product(pe, o, (w_hi[:, c, cols], w_lo[:, c, cols]),
                               (ctx_hi[:, c, :], ctx_lo[:, c, :]), c == 0, c == DC - 1)
        if p % 4 == 3:
            mm.then_inc(ready, 1)


def halves(hi, kv32):
    for h in range(2):
        rows = slice(h * DK, (h + 1) * DK)
        yield (hi[rows, :, :, h, :].rearrange("r p b k -> r (p b) k"),
               kv32[rows, :, :].rearrange("r p (b k) -> r (p b) k", b=GB))


def scores_phase(nc, xT, ctxT, maskT, wk, wqT, wv, wo, bk, bq, bv, sel_bc_d, scores_d,
                 wv_hi, wv_lo, wo_hi, wo_lo, bkv, ctx32, ctx_hi, ctx_lo, kv32, kv_hi, kv_lo,
                 s32, sel_bc, score_max, least):
    with ExitStack() as ctx:
        def sb(name, shape, dt=F32):
            return ctx.enter_context(nc.sbuf_tensor(name, shape, dt))

        def sem(name):
            return ctx.enter_context(nc.semaphore(name))

        def bank(name):
            return ctx.enter_context(nc.psum_tensor(name, [P, 512], F32))

        wk_hi, wk_lo = sb("wk_hi", [P, DC, HD], F16), sb("wk_lo", [P, DC, HD], F16)
        wq_hi, wq_lo = sb("wq_hi", [P, NP, D], F16), sb("wq_lo", [P, NP, D], F16)
        w32 = sb("w32", [P, 2, 1024])
        bq32, bq16 = sb("bq32", [P, NP]), sb("bq16", [P, NP, 2], F16)
        x32 = sb("x32", [P, 2, DC, TT])
        x_hi, x_lo = sb("x_hi", [P, 2, DC, TT], F16), sb("x_lo", [P, 2, DC, TT], F16)
        g_hi, g_lo = sb("g_hi", [P, NP, DC, GB, P], F16), sb("g_lo", [P, NP, DC, GB, P], F16)
        c_raw, c_bias = sb("c_raw", [P, NP * GB]), sb("c_bias", [P, NP * GB])
        mask32, mask_add = sb("mask32", [P, T], I32), sb("mask_add", [P, 2, T])
        tile_max, mask_min = sb("tile_max", [P, 2]), sb("mask_min", [P, 1])

        ps_s = [bank(f"ps_s{i}") for i in range(SBANKS)]
        ps_g = [bank(f"ps_g{i}") for i in range(GBANKS)]
        ps_k = [bank(f"ps_k{i}") for i in range(2)]

        w_in = [sem(f"w_in{i}") for i in range(2)]
        w_hi_done, w_lo_done = sem("w_hi_done"), sem("w_lo_done")
        small_in, bq_done = sem("small_in"), sem("bq_done")
        ctx_in, ctx_hi_done, ctx_lo_done = sem("ctx_in"), sem("ctx_hi_done"), sem("ctx_lo_done")
        x_in = [sem(f"x_in{i}") for i in range(2)]
        x_hi_done, x_lo_done = sem("x_hi_done"), sem("x_lo_done")
        mask_in, mask_ready = sem("mask_in"), sem("mask_ready")
        zeroed = sem("zeroed")
        k_summed, k32_done = sem("k_summed"), sem("k32_done")
        k_hi_done, k_lo_done = sem("k_hi_done"), sem("k_lo_done")
        c_summed, c_ready, c_rawed = sem("c_summed"), sem("c_ready"), sem("c_rawed")
        g_summed, g_hi_done, g_lo_done = sem("g_summed"), sem("g_hi_done"), sem("g_lo_done")
        s_summed, s_out, s_masked = sem("s_summed"), sem("s_out"), sem("s_masked")
        least_steps, max_steps = sem("least_steps"), sem("max_steps")
        s_stored = [sem(f"s_stored{i}") for i in range(2)]
        first_weights = [(wk, wk_hi, wk_lo), (wqT, wq_hi, wq_lo)]
        later_weights = [(wv, wv_hi, wv_lo), (wo, wo_hi, wo_lo)]

        def chunk(i):
            w, hi, lo = (first_weights + later_weights)[i // 4]
            c = i % 4
            flat = lambda a: a.rearrange("p c n -> p (c n)")[:, c * 1024:(c + 1) * 1024]
            return w[c], flat(hi[:, :, :]), flat(lo[:, :, :])

        block = ctx.enter_context(nc.Block())

        @block.sync
        def _(sp):
            def load_weight(i):
                if i >= 2:
                    sp.wait_ge(w_lo_done, i - 1)
                sp.dma_start(w32[:, i % 2, :], chunk(i)[0]).then_inc(w_in[i % 2], 16)

            def load_sel():
                for i in range(2):
                    sp.wait_ge(w_lo_done, 16)
                    sp.dma_start(w32[:, i, :], sel_bc_d[i]).then_inc(w_in[i], 16)

            def load_ctx(g):
                sp.dma_start(ctx32[:, :, :], ctxT[:, :, bass.ds(g * KC, KC)].rearrange("c p k -> p c k"))\
                  .then_inc(ctx_in, 16)

            def load_x(n, b, u):
                sp.wait_ge(x_lo_done, n + 1)
                sp.dma_start(x32[:, u % 2, :, :],
                             xT[bass.ds(b, 1), :, :, (u % 2) * TT:(u % 2 + 1) * TT]
                             .rearrange("a c p t -> p (a c) t")).then_inc(x_in[u % 2], 16)

            def load_mask(b):
                sp.wait_ge(mask_ready, b + 1)
                for h in range(2):
                    sp.dma_start(mask32[h * NK:(h + 1) * NK, :],
                                 maskT[bass.ds(b, 1), :, :].rearrange("a k t -> (a k) t")).then_inc(mask_in, 16)

            def store_scores(n, u):
                sp.wait_ge(s_masked, (n + 2) * NP)
                sp.dma_start(scores_d[bass.ds(n, 1), :, :].rearrange("a p n -> p (a n)"),
                             s32[:, u % 2, :, :].rearrange("r p t -> r (p t)")).then_inc(s_stored[u % 2], 16)

            for i in range(2):
                sp.sem_inc(s_stored[i], 16)
            load_ctx(0)
            for half, w in enumerate((bk, bv)):
                sp.dma_start(bkv[:, half, :], w).then_inc(small_in, 16)
            sp.dma_start(bq32[:, :], bq).then_inc(small_in, 16)
            for i in range(8):
                load_weight(i)
            load_mask(0)
            load_x(0, 0, 0)
            load_x(1, 0, 1)

            def group(g, last):
                load_mask(g * GB + 1)
                sp.wait_ge(ctx_lo_done, g + 1)
                load_ctx(g + 1)
                for u in range(UNITS):
                    if not (last and u >= UNITS - 2):
                        load_x(g * UNITS + u + 2, g * GB + (u + 2) // UB, u)
                    if u == 2 and not last:
                        load_mask(g * GB + 2)
                    if last and u < 2:
                        for i in range(8 + 4 * u, 12 + 4 * u):
                            load_weight(i)
                    if last and u == 2:
                        load_sel()
                    if not (last and u >= UNITS - UB):
                        store_scores(g * UNITS + u, u)

            with sp.Fori(0, NG - 1) as g:
                group(g, False)
            group(NG - 1, True)
            for i in range(2):
                sp.wait_ge(s_stored[i], 16 + 16 * (NU // 2 - 1))

        @block.tensor
        def _(pe):
            pe.sem_inc(s_summed, 2 * NP)

            def project(g):
                pe.wait_ge(ctx_lo_done, g + 1)
                pe.wait_ge(c_ready, g + 1)
                project_heads(pe, ps_k, wk_hi, wk_lo, ctx_hi, ctx_lo, k_summed)

            def bias(g):
                pe.wait_ge(k_hi_done, 2 * g + 2)
                pe.wait_ge(k_lo_done, 2 * g + 2)
                for p in range(NP):
                    for b in range(GB):
                        o = ps_k[0][:, 2 * (GB * p + b):2 * (GB * p + b) + 2]
                        for k, half in enumerate((kv_hi, kv_lo)):
                            mm = pe.matmul(o, half[:, p, b, :, :].rearrange("r h k -> r (h k)"), bq16[:, p, :],
                                           start=(k == 0), stop=(k == 1))
                mm.then_inc(c_summed, 1)

            def fold_q(g):
                for i in range(GT):
                    p, dp = i // 2, i % 2
                    pe.wait_ge(g_lo_done, g * GT + i + 1)
                    k2 = tuple(k[:, p, :, :, :].rearrange("r b h k -> r (b h k)") for k in (kv_hi, kv_lo))
                    for j in range(2):
                        cols = slice((2 * dp + j) * P, (2 * dp + j + 1) * P)
                        mm = split_product(pe, ps_g[i % GBANKS][:, j * GB * P:(j + 1) * GB * P],
                                           (wq_hi[:, p, cols], wq_lo[:, p, cols]), k2, True, True)
                    mm.then_inc(g_summed, 1)

            def scores(g, u):
                n, b = g * UNITS + u, u // UB
                pe.wait_ge(x_lo_done, n + 3)
                for p in range(NP):
                    if u == 0:
                        pe.wait_ge(g_lo_done, g * GT + 2 * p + 2 + GBANKS)
                    pe.wait_ge(s_out, n * NP + p + 1)
                    for c in range(DC):
                        mm = split_product(pe, ps_s[p % SBANKS][:, :],
                                           (g_hi[:, p, c, b, :], g_lo[:, p, c, b, :]),
                                           (x_hi[:, u % 2, c, :], x_lo[:, u % 2, c, :]), c == 0, c == DC - 1)
                    mm.then_inc(s_summed, 1)

            def group(g, last):
                bias(g)
                fold_q(g)
                for u in range(UNITS):
                    scores(g, u)
                    if u == UNITS - 2 and not last:
                        project(g + 1)

            pe.wait_ge(w_lo_done, 4)
            project(0)
            pe.wait_ge(w_lo_done, 8)
            pe.wait_ge(bq_done, 2)
            with pe.Fori(0, NG - 1) as g:
                group(g, False)
            group(NG - 1, True)

        @block.scalar
        def _(act):
            act.sem_inc(s_out, SBANKS)

            def split_weight(i):
                act.wait_ge(w_in[i % 2], 16 * (i // 2 + 1))
                act.activation(chunk(i)[1], w32[:, i % 2, :], ACT.Copy, scale=W_SCALE).then_inc(w_hi_done, 1)

            def split_ctx(g):
                act.wait_ge(ctx_in, 16 * (g + 1))
                act.activation(ctx_hi[:, :, :], ctx32[:, :, :], ACT.Copy, scale=CTX_SCALE).then_inc(ctx_hi_done, 1)

            def round_x(g, u):
                act.wait_ge(x_in[u % 2], g * (8 * UNITS) + 16 * (u // 2 + 1))
                act.wait_ge(s_summed, (g * UNITS + u + 1) * NP)
                act.activation(x_hi[:, u % 2, :, :], x32[:, u % 2, :, :], ACT.Copy, scale=X_SCALE)\
                   .then_inc(x_hi_done, 1)

            def round_k(g):
                if not (isinstance(g, int) and g == 0):
                    act.wait_ge(k_lo_done, 2 * g)
                for p in range(NP):
                    if p % 4 == 0:
                        act.wait_ge(k_summed, 2 * g + p // 4 + 1)
                    act.activation(kv32[:, p, :], ps_k[p // 4][:, (p % 4) * KC:(p % 4 + 1) * KC], ACT.Identity,
                                   bias=bkv[:, 0, p:p + 1], scale=1 / (W_SCALE * CTX_SCALE)).then_inc(k32_done, 1)
                act.wait_ge(k32_done, NP * (g + 1))
                for o, i in halves(kv_hi, kv32):
                    act.activation(o, i, ACT.Copy, scale=K_SCALE).then_inc(k_hi_done, 1)

            def round_g(g):
                act.wait_ge(s_summed, (g * UNITS + 2) * NP)
                for i in range(GT):
                    p, dp = i // 2, i % 2
                    act.wait_ge(g_summed, g * GT + i + 1)
                    act.activation(g_hi[:, p, 2 * dp:2 * dp + 2, :, :].rearrange("r c b k -> r (c b k)"),
                                   ps_g[i % GBANKS][:, :], ACT.Copy, scale=G_SCALE / (W_SCALE * K_SCALE))\
                       .then_inc(g_hi_done, 1)

            def scores_out(g, u):
                n = g * UNITS + u
                act.wait_ge(s_stored[u % 2], g * (8 * UNITS) + 16 * (u // 2 + 1))
                if u == 0:
                    act.wait_ge(c_ready, g + 2)
                for p in range(NP):
                    act.wait_ge(s_summed, n * NP + p + 1 + 2 * NP)
                    k = GB * p + u // UB
                    act.activation(s32[:, u % 2, p, :], ps_s[p % SBANKS][:, :], ACT.Identity, bias=c_bias[:, k:k + 1],
                                   scale=1 / (G_SCALE * X_SCALE)).then_inc(s_out, 1)

            def group(g, last):
                round_g(g)
                for u in range(UNITS):
                    if not (last and u == UNITS - 1):
                        round_x(g, u + 1)
                    scores_out(g, u)
                    if u == 1:
                        act.wait_ge(k_summed, 2 * g + 2)
                        split_ctx(g + 1)
                    if u == UNITS - 2 and not last:
                        act.wait_ge(g_summed, (g + 1) * GT)
                        round_k(g + 1)
                    if last and u < 2:
                        for i in range(8 + 4 * u, 12 + 4 * u):
                            split_weight(i)
                    if last and u == 2:
                        for i in range(2):
                            act.wait_ge(w_in[i], 16 * 9)
                            act.activation(sel_bc[:, 4 * i:4 * i + 4, :, :].rearrange("r p t k -> r (p t k)"),
                                           w32[:, i, :], ACT.Copy)

            split_ctx(0)
            act.wait_ge(small_in, 48)
            act.activation(bq16[:, :, 0], bq32[:, :], ACT.Copy, scale=W_SCALE).then_inc(bq_done, 1)
            for i in range(8):
                split_weight(i)
                if i == 3:
                    act.wait_ge(zeroed, 2)
            round_k(0)
            round_x(0, 0)
            with act.Fori(0, NG - 1) as g:
                group(g, False)
            group(NG - 1, True)

        @block.vector
        def _(dve):
            dve.sem_inc(x_lo_done, 2)
            dve.sem_inc(mask_ready, 1)
            dve.sem_inc(g_lo_done, GBANKS)
            dve.sem_inc(s_masked, NP)
            dve.sem_inc(c_ready, 1)
            dve.memset(kv_hi[:, :, :, :, :], 0.0).then_inc(zeroed, 1)
            dve.memset(kv_lo[:, :, :, :, :], 0.0).then_inc(zeroed, 1)
            dve.memset(score_max[:, :], MASKED).then_inc(max_steps, 1)
            dve.memset(tile_max[:, :], MASKED).then_inc(max_steps, 1)
            dve.memset(least[:, :], 0.0).then_inc(least_steps, 1)
            dve.wait_ge(least_steps, 1)

            def split_weight(i):
                dve.wait_ge(w_hi_done, i + 1)
                _, hi, lo = chunk(i)
                dve.scalar_tensor_tensor(lo, w32[:, i % 2, :], W_SCALE, hi, ALU.mult, ALU.subtract)\
                   .then_inc(w_lo_done, 1)

            def split_ctx(g):
                dve.wait_ge(ctx_hi_done, g + 1)
                dve.scalar_tensor_tensor(ctx_lo[:, :, :], ctx32[:, :, :], CTX_SCALE, ctx_hi[:, :, :],
                                         ALU.mult, ALU.subtract).then_inc(ctx_lo_done, 1)

            def split_x(g, u):
                dve.wait_ge(x_hi_done, g * UNITS + u + 1)
                dve.scalar_tensor_tensor(x_lo[:, u % 2, :, :], x32[:, u % 2, :, :], X_SCALE, x_hi[:, u % 2, :, :],
                                         ALU.mult, ALU.subtract).then_inc(x_lo_done, 1)

            def split_k(g):
                dve.wait_ge(k_hi_done, 2 * g + 2)
                for (o, i), (hi, _) in zip(halves(kv_lo, kv32), halves(kv_hi, kv32)):
                    dve.scalar_tensor_tensor(o, i, K_SCALE, hi, ALU.mult, ALU.subtract).then_inc(k_lo_done, 1)

            def split_g(g):
                for i in range(GT):
                    p, dp = i // 2, i % 2
                    at = lambda a: a[:, p, 2 * dp:2 * dp + 2, :, :].rearrange("r c b k -> r (c b k)")
                    dve.wait_ge(g_hi_done, g * GT + i + 1)
                    dve.scalar_tensor_tensor(at(g_lo), ps_g[i % GBANKS][:, :], G_SCALE / (W_SCALE * K_SCALE), at(g_hi),
                                             ALU.mult, ALU.subtract).then_inc(g_lo_done, 1)

            def bias(g):
                dve.wait_ge(c_summed, g + 1)
                dve.tensor_reduce(c_raw[:, :], ps_k[0][:, 0:2 * NP * GB].rearrange("r (n k) -> r n k", k=2),
                                  axis=AX.X, op=ALU.add).then_inc(c_rawed, 1)
                dve.wait_ge(c_rawed, g + 1)
                dve.wait_ge(s_out, g * UNITS * NP + SBANKS)
                dve.tensor_scalar(c_bias[:, :], c_raw[:, :], 1 / (W_SCALE * K_SCALE), None, ALU.mult)\
                   .then_inc(c_ready, 1)

            def mask(g, j):
                b = g * GB + j
                dve.wait_ge(mask_in, 32 * (b + 1))
                if j == 0:
                    dve.wait_ge(s_masked, (g * UNITS + 1) * NP)
                dve.tensor_scalar(mask_add[:, j, :], mask32[:, :], -MASKED, MASKED, ALU.mult, ALU.add)\
                   .then_inc(mask_ready, 1)
                dve.wait_ge(mask_ready, b + 2)
                dve.tensor_reduce(mask_min[:, :], mask_add[:, j, :], axis=AX.X, op=ALU.min).then_inc(least_steps, 1)
                dve.wait_ge(least_steps, 2 * b + 2)
                dve.tensor_tensor(least[:, :], least[:, :], mask_min[:, :], ALU.min).then_inc(least_steps, 1)

            def raise_max(k, p):
                dve.wait_ge(s_masked, k + NP)
                dve.wait_ge(max_steps, k + 2)
                dve.tensor_tensor(score_max[:, :], score_max[:, :], tile_max[:, (p + 1) % 2:(p + 1) % 2 + 1],
                                  ALU.max).then_inc(max_steps, 1)

            def mask_scores(g, u):
                n, j, t0 = g * UNITS + u, u // UB, (u % UB) * TT
                for p in range(NP):
                    dve.wait_ge(s_out, n * NP + p + 1 + SBANKS)
                    raise_max(n * NP + p, p)
                    dve.tensor_tensor_reduce(s32[:, u % 2, p, :], s32[:, u % 2, p, :], mask_add[:, j, t0:t0 + TT],
                                             1.0, MASKED, ALU.add, ALU.max, tile_max[:, p % 2:p % 2 + 1])\
                       .then_inc(s_masked, 1)

            def group(g, last):
                bias(g)
                split_g(g)
                for u in range(UNITS):
                    if not (last and u == UNITS - 1):
                        split_x(g, u + 1)
                    if u % UB == 0:
                        mask(g, u // UB)
                    mask_scores(g, u)
                    if u == 1:
                        split_ctx(g + 1)
                    if u == UNITS - 2 and not last:
                        split_k(g + 1)
                    if last and u < 2:
                        for i in range(8 + 4 * u, 12 + 4 * u):
                            split_weight(i)

            split_ctx(0)
            dve.wait_ge(bq_done, 1)
            dve.scalar_tensor_tensor(bq16[:, :, 1], bq32[:, :], W_SCALE, bq16[:, :, 0], ALU.mult, ALU.subtract)\
               .then_inc(bq_done, 1)
            for i in range(8):
                split_weight(i)
            split_k(0)
            split_x(0, 0)
            with dve.Fori(0, NG - 1) as g:
                group(g, False)
            group(NG - 1, True)

            raise_max(NU * NP, NP)


def output_phase(nc, x, ctxT, scores_d, bo, gamma, beta, sel_sum_d, part_d, out,
                 wv_hi, wv_lo, wo_hi, wo_lo, bkv, ctx32, ctx_hi, ctx_lo, kv32, kv_hi, kv_lo,
                 s32, sel_sum, sel_bc, score_max, least, key_max, neg_max):
    HT = TT // 2

    with ExitStack() as ctx:
        def sb(name, shape, dt=F32):
            return ctx.enter_context(nc.sbuf_tensor(name, shape, dt))

        def sem(name):
            return ctx.enter_context(nc.semaphore(name))

        def bank(name):
            return ctx.enter_context(nc.psum_tensor(name, [P, 512], F32))

        u_hi, u_lo = sb("u_hi", [P, GB, NP, D], F16), sb("u_lo", [P, GB, NP, D], F16)
        p_hi, p_lo = sb("p_hi", [P, 2, NP, TT], F16), sb("p_lo", [P, 2, NP, TT], F16)
        y32 = sb("y32", [P, UNITS, TB, D])
        gamma_b, beta_b, bo_b = sb("gamma_b", [P, D]), sb("beta_b", [P, D]), sb("bo_b", [P, D])
        part = sb("part", [P, 2])
        den, r32, rest = sb("den", [P, HT]), sb("r32", [P, HT]), sb("rest", [P, HT])
        r_hi, r_mid, r_all = sb("r_hi", [P, HT], BF16), sb("r_mid", [P, HT], BF16), sb("r_all", [P, HT], BF16)
        stats, mean_var = sb("stats", [P, TB, 6]), sb("mean_var", [P, TB, 2])
        var_eps, rstd, minus_half = sb("var_eps", [P, TB]), sb("rstd", [P, TB]), sb("minus_half", [P, 1])
        ln_eps = sb("ln_eps", [P, 1])

        ps_sum = bank("ps_sum")
        ps_bc = [bank(f"ps_bc{i}") for i in range(2)]
        ps_o = [bank(f"ps_o{i}") for i in range(2)]
        ps_u = [bank(f"ps_u{i}") for i in range(2)]

        sum_in, affine_in, consts_done = sem("sum_in"), sem("affine_in"), sem("consts_done")
        key_max_done, max_local, max_global, max_done = (sem(n) for n in (
            "key_max_done", "max_local", "max_global", "max_done"))
        ctx_in, ctx_hi_done, ctx_lo_done = sem("ctx2_in"), sem("ctx2_hi_done"), sem("ctx2_lo_done")
        s_in = [sem(f"s_in{i}") for i in range(2)]
        x_in = [sem(f"xres_in{i}") for i in range(UNITS)]
        v_summed, v32_done = sem("v_summed"), sem("v32_done")
        v_hi_done, v_lo_done = sem("v_hi_done"), sem("v_lo_done")
        u_summed, u_hi_done, u_lo_done = sem("u_summed"), sem("u_hi_done"), sem("u_lo_done")
        exp_done, e_summed = sem("exp_done"), sem("e_summed")
        den_done, r_done, r_hi_done = sem("den_done"), sem("r_done"), sem("r_hi_done")
        rest_done, r_mid_done, r_all_done = sem("rest_done"), sem("r_mid_done"), sem("r_all_done")
        r_spread, p_scaled = sem("r_spread"), sem("p_scaled")
        p_hi_done, p_lo_done = sem("p_hi_done"), sem("p_lo_done")
        o_summed, y_added, mean_done = sem("o_summed"), sem("y_added"), sem("mean_done")
        eps_added, rstd_done = sem("eps_added"), sem("rstd_done")
        normed, scaled, shifted, bo_added = sem("normed"), sem("scaled"), sem("shifted"), sem("bo_added")
        y_stored = [sem(f"y_stored{i}") for i in range(UNITS)]

        def tokens(a, b, u):
            t0 = (u % UB) * TT
            return a[bass.ds(b, 1), t0:t0 + TT, :].rearrange("a (n p) d -> p (a n) d", p=P)

        def u_tile(g, j):
            return g * (2 * NP) + NP + j, 1 - j // NP, j % NP

        block = ctx.enter_context(nc.Block())

        @block.sync
        def _(sp):
            def load_scores(n, u):
                sp.wait_ge(p_lo_done, 4 * n + 4)
                sp.dma_start(s32[:, u % 2, :, :].rearrange("r p t -> r (p t)"),
                             scores_d[bass.ds(n - UB, 1), :, :].rearrange("a p n -> p (a n)"))\
                  .then_inc(s_in[u % 2], 16)

            def load_x(g, u):
                s = u % UNITS
                sp.wait_ge(y_stored[s], 16 * g + 16 * (u // UNITS) + 16)
                sp.dma_start(y32[:, s, :, :], tokens(x, g * GB + u // UB, u)).then_inc(x_in[s], 16)

            def load_ctx(g):
                sp.dma_start(ctx32[:, :, :], ctxT[:, :, bass.ds(g * KC, KC)].rearrange("c p k -> p c k"))\
                  .then_inc(ctx_in, 16)

            def store_y(g, u):
                sp.wait_ge(shifted, (g * UNITS + u + 1) * TB)
                sp.dma_start(tokens(out, g * GB + u // UB, u), y32[:, u, :, :]).then_inc(y_stored[u], 16)

            for i in range(UNITS):
                sp.sem_inc(y_stored[i], 16)
            sp.dma_start(sel_sum[:, :, :], sel_sum_d).then_inc(sum_in, 16)
            sp.dma_start(part[:, :], part_d).then_inc(sum_in, 16)
            for to, of in ((gamma_b, gamma), (beta_b, beta), (bo_b, bo)):
                sp.dma_start(to[:, :], of.rearrange("(a d) -> a d", a=1).to_broadcast([P, D])).then_inc(affine_in, 16)
            load_x(0, 0)
            load_x(0, 1)

            def group(g, last):
                if not last:
                    sp.wait_ge(ctx_lo_done, g + 1)
                    load_ctx(g + 1)
                for u in range(UNITS):
                    if not (last and u >= UNITS - 2):
                        load_scores(g * UNITS + u + 2, u)
                        load_x(g, u + 2)
                    store_y(g, u)

            with sp.Fori(0, NG - 1) as g:
                group(g, False)
            group(NG - 1, True)
            for i in range(UNITS):
                sp.wait_ge(y_stored[i], 16 + 16 * NG)

        @block.tensor
        def _(pe):
            pe.sem_inc(o_summed, 2 * TB)

            def fold_o(g, j):
                k, b, p = u_tile(g, j)
                if j % NP == 0:
                    group_of_v = g + 1 if j else g
                    pe.wait_ge(v_hi_done, 2 * group_of_v + 2)
                    pe.wait_ge(v_lo_done, 2 * group_of_v + 2)
                pe.wait_ge(u_lo_done, k + 1)
                v2 = tuple(v[:, p, b, :, :].rearrange("r h k -> r (h k)") for v in (kv_hi, kv_lo))
                split_product(pe, ps_u[p % 2][:, :], v2, (wo_hi[:, p, :], wo_lo[:, p, :]), True, True)\
                    .then_inc(u_summed, 1)

            def sums(n, s):
                pe.wait_ge(exp_done, 2 * n + 2)
                pe.wait_ge(den_done, n + 1)
                for i in range(4):
                    for q in range(4):
                        th, p = q // 2, 4 * (q % 2) + i
                        mm = pe.matmul(ps_sum[32 * q:32 * q + 32, 0:HT], sel_sum[:, i, :],
                                       s32[:, s, p, th * HT:(th + 1) * HT],
                                       start=(i == 0), stop=(i == 3), skip_group_check=True)
                mm.then_inc(e_summed, 1)

            def spread(n, p):
                if p == 0:
                    pe.wait_ge(r_all_done, n + 1)
                pe.wait_ge(p_scaled, n * NP + p + 1)
                for th in range(2):
                    mm = pe.matmul(ps_bc[p % 2][:, th * HT:(th + 1) * HT], sel_bc[:, p, th, :], r_all[:, :],
                                   start=True, stop=True)
                mm.then_inc(r_spread, 1)

            def project(g, pairs):
                if pairs[0] == 0:
                    pe.wait_ge(u_lo_done, (g - 1) * (2 * NP) + 2 * NP + 2)
                    pe.wait_ge(ctx_lo_done, g + 1)
                project_heads(pe, ps_u, wv_hi, wv_lo, ctx_hi, ctx_lo, v_summed, pairs)

            def unit(g, u, last):
                n, s, b = g * UNITS + u, u % 2, u // UB
                more = not (last and u == UNITS - 1)
                spreads = {(1, 0): 0, (1, 3): 1, (1, 5): 2, (2, 0): 3, (2, 3): 4, (2, 5): 5, (3, 0): 6, (3, 3): 7}
                folds = [{(t, p): 2 * t + p // 4 for t in range(TB) for p in (2, 6)}, {},
                         {(2, 1): 8, (2, 6): 9, (3, 1): 10, (3, 5): 11}, {(t, 4): 12 + t for t in range(TB)}][u]
                if more:
                    sums(n + 1, (u + 1) % 2)
                for t in range(TB):
                    pe.wait_ge(y_added, n * TB + t + 1)
                    for p in range(NP):
                        if more and (t, p) in spreads:
                            spread(n + 1, spreads[t, p])
                        if (t, p) in folds and not (last and u > 0):
                            fold_o(g, folds[t, p])
                        if u == 1 and not last and p % 4 == 2:
                            project(g + 1, [2 * t + p // 4])
                        if t == 0 and p % 2 == 0:
                            pe.wait_ge(p_lo_done, 4 * n + p // 2 + 1 + 8)
                        if t == 0 and u % UB == 0:
                            pe.wait_ge(u_lo_done, g * (2 * NP) + b * NP + p + 1 + 2)
                        cols = slice(t * P, (t + 1) * P)
                        mm = split_product(pe, ps_o[t % 2][:, :], (p_hi[:, s, p, cols], p_lo[:, s, p, cols]),
                                           (u_hi[:, b, p, :], u_lo[:, b, p, :]), p == 0, p == NP - 1)
                    mm.then_inc(o_summed, 1)

            def group(g, last):
                for u in range(UNITS):
                    unit(g, u, last)

            project_heads(pe, ps_u, wv_hi, wv_lo, ctx_hi, ctx_lo, v_summed)
            pe.wait_ge(sum_in, 32)
            sums(0, 0)
            for p in range(NP):
                fold_o(-1, NP + p)
                spread(0, p)
            with pe.Fori(0, NG - 1) as g:
                group(g, False)
            group(NG - 1, True)

        @block.scalar
        def _(act):
            def exps(n, u, half):
                if not isinstance(n, int) or n >= UB:
                    act.wait_ge(s_in[u % 2], 8 * n - 8 * (u % 2))
                e = s32[:, u % 2, 4 * half:4 * half + 4, :]
                act.activation(e, e, ACT.Exp, bias=neg_max[:, 0:1]).then_inc(exp_done, 1)

            def round_ctx(g):
                act.wait_ge(ctx_in, 16 * g)
                act.activation(ctx_hi[:, :, :], ctx32[:, :, :], ACT.Copy, scale=CTX_SCALE).then_inc(ctx_hi_done, 1)

            def round_v(g):
                if not (isinstance(g, int) and g == 0):
                    act.wait_ge(v_lo_done, 2 * g)
                    act.wait_ge(u_summed, (g - 1) * (2 * NP) + 2 * NP)
                for p in range(NP):
                    if p % 4 == 0:
                        act.wait_ge(v_summed, 2 * g + p // 4 + 1)
                    act.activation(kv32[:, p, :], ps_u[p // 4][:, (p % 4) * KC:(p % 4 + 1) * KC], ACT.Identity,
                                   bias=bkv[:, 1, p:p + 1], scale=1 / (W_SCALE * CTX_SCALE)).then_inc(v32_done, 1)
                act.wait_ge(v32_done, NP * (g + 1))
                for o, i in halves(kv_hi, kv32):
                    act.activation(o, i, ACT.Copy, scale=V_SCALE).then_inc(v_hi_done, 1)

            def round_u(g, *js):
                for j in js:
                    k, b, p = u_tile(g, j)
                    if j % NP == 0 and not (isinstance(g, int) and g < 0):
                        act.wait_ge(o_summed, g * (UNITS * TB) + (2 * TB if j == 0 else 4 * TB))
                    act.wait_ge(u_summed, k + 1)
                    act.activation(u_hi[:, b, p, :], ps_u[p % 2][:, :], ACT.Copy,
                                   scale=U_SCALE / (W_SCALE * V_SCALE)).then_inc(u_hi_done, 1)

            def round_r(n):
                act.wait_ge(r_done, n + 1)
                act.activation(r_hi[:, :], r32[:, :], ACT.Copy).then_inc(r_hi_done, 1)
                act.wait_ge(rest_done, n + 1)
                act.activation(r_mid[:, :], rest[:, :], ACT.Copy).then_inc(r_mid_done, 1)

            def round_p(n, s, k):
                if k == 0:
                    act.wait_ge(o_summed, TB * n + TB)
                act.wait_ge(p_scaled, n * NP + 2 * k + 2 + 2)
                act.activation(p_hi[:, s, 2 * k:2 * k + 2, :], s32[:, s, 2 * k:2 * k + 2, :], ACT.Copy)\
                   .then_inc(p_hi_done, 1)

            def group(g, last):
                for u in range(UNITS):
                    n, s = g * UNITS + u, (u + 1) % 2
                    more, more2 = not (last and u == UNITS - 1), not (last and u >= UNITS - 2)
                    halve = lambda k: round_p(n + 1, s, k) if more else None
                    expo = lambda half: exps(n + 2, u, half) if more2 else None
                    fold = lambda *js: round_u(g, *js) if not (last and u > 0) else None
                    if more:
                        round_r(n + 1)
                    if u == 0:
                        fold(0, 1, 2)
                        halve(0)
                        fold(3, 4)
                        halve(1)
                        fold(5)
                        expo(0)
                        fold(6)
                        halve(2)
                        expo(1)
                        fold(7)
                        halve(3)
                        if not last:
                            act.wait_ge(v_summed, 2 * g + 2)
                            round_ctx(g + 1)
                    elif u == 1:
                        halve(0)
                        halve(1)
                        expo(0)
                        halve(2)
                        expo(1)
                        halve(3)
                    elif u == 2:
                        if not last:
                            round_v(g + 1)
                        halve(0)
                        fold(8)
                        halve(1)
                        expo(0)
                        fold(9)
                        halve(2)
                        expo(1)
                        fold(10, 11)
                        halve(3)
                    else:
                        fold(12)
                        halve(0)
                        fold(13)
                        halve(1)
                        expo(0)
                        fold(14)
                        halve(2)
                        expo(1)
                        fold(15)
                        halve(3)

            act.wait_ge(max_done, 1)
            exps(0, 0, 0)
            exps(0, 0, 1)
            round_v(0)
            round_r(0)
            for k in range(4):
                round_u(-1, NP + 2 * k, NP + 2 * k + 1)
                round_p(0, 0, k)
            exps(1, 1, 0)
            exps(1, 1, 1)
            with act.Fori(0, NG - 1) as g:
                group(g, False)
            group(NG - 1, True)

        @block.vector
        def _(dve):
            dve.sem_inc(u_lo_done, 2)
            dve.sem_inc(den_done, 1)
            dve.sem_inc(p_scaled, 2)
            dve.sem_inc(p_lo_done, 8)
            dve.sem_inc(y_added, 2)
            dve.sem_inc(ctx_lo_done, 1)

            def split_ctx(g):
                dve.wait_ge(ctx_hi_done, g)
                dve.scalar_tensor_tensor(ctx_lo[:, :, :], ctx32[:, :, :], CTX_SCALE, ctx_hi[:, :, :],
                                         ALU.mult, ALU.subtract).then_inc(ctx_lo_done, 1)

            def split_v(g):
                dve.wait_ge(v_hi_done, 2 * g + 2)
                for (o, i), (hi, _) in zip(halves(kv_lo, kv32), halves(kv_hi, kv32)):
                    dve.scalar_tensor_tensor(o, i, V_SCALE, hi, ALU.mult, ALU.subtract).then_inc(v_lo_done, 1)

            def split_u(g, *js):
                for j in js:
                    k, b, p = u_tile(g, j)
                    dve.wait_ge(u_hi_done, k + 1)
                    dve.scalar_tensor_tensor(u_lo[:, b, p, :], ps_u[p % 2][:, :], U_SCALE / (W_SCALE * V_SCALE),
                                             u_hi[:, b, p, :], ALU.mult, ALU.subtract).then_inc(u_lo_done, 1)

            def invert(n):
                dve.wait_ge(e_summed, n + 1)
                dve.tensor_scalar(den[:, :], ps_sum[:, 0:HT], TINY, None, ALU.add).then_inc(den_done, 1)
                dve.wait_ge(den_done, n + 2)
                dve.reciprocal(r32[:, :], den[:, :]).then_inc(r_done, 1)
                dve.wait_ge(r_hi_done, n + 1)
                dve.scalar_tensor_tensor(rest[:, :], r_hi[:, :], part[:, 0:1], r32[:, :], ALU.mult, ALU.add)\
                   .then_inc(rest_done, 1)
                dve.wait_ge(r_mid_done, n + 1)
                if not (isinstance(n, int) and n == 0):
                    dve.wait_ge(r_spread, n * NP)
                dve.scalar_tensor_tensor(r_all[:, :], r_mid[:, :], part[:, 1:2], rest[:, :], ALU.mult, ALU.add)\
                   .then_inc(r_all_done, 1)

            def scale_p(n, s, p):
                dve.wait_ge(r_spread, n * NP + p + 1)
                e = s32[:, s, p, :]
                dve.tensor_tensor(e, e, ps_bc[p % 2][:, :], ALU.mult).then_inc(p_scaled, 1)

            def split_p(n, s, k):
                dve.wait_ge(p_hi_done, 4 * n + k + 1)
                at = lambda a: a[:, s, 2 * k:2 * k + 2, :].rearrange("r p t -> r (p t)")
                dve.tensor_tensor(at(p_lo), at(s32), at(p_hi), ALU.subtract).then_inc(p_lo_done, 1)

            def residual(g, u, t):
                n = g * UNITS + u
                k = n * TB + t
                if t == 0:
                    dve.wait_ge(bo_added, n + 1)
                dve.wait_ge(o_summed, k + 1 + 2 * TB)
                y = y32[:, u, t, :]
                dve.scalar_tensor_tensor(y, ps_o[t % 2][:, :], 1 / (P_SCALE * U_SCALE), y, ALU.mult, ALU.add)\
                   .then_inc(y_added, 1)
                dve.wait_ge(y_added, k + 3)
                dve.bn_stats(stats[:, t, :], y)
                dve.drain()
                dve.bn_aggr(mean_var[:, t, :], stats[:, t, :]).then_inc(mean_done, 1)

            def norm(g, u, t):
                dve.wait_ge(rstd_done, (g * UNITS + u) * TB + t + 1)
                y = y32[:, u, t, :]
                dve.tensor_scalar(y, y, mean_var[:, t, 0:1], rstd[:, t:t + 1], ALU.subtract, ALU.mult)\
                   .then_inc(normed, 1)

            def group(g, last):
                for u in range(UNITS):
                    n, s = g * UNITS + u + 1, (u + 1) % 2
                    more = not (last and u == UNITS - 1)
                    scale = lambda *ps: [scale_p(n, s, p) for p in ps] if more else None
                    split = lambda *ks: [split_p(n, s, k) for k in ks] if more else None
                    fold = lambda *js: split_u(g, *js) if not (last and u > 0) else None
                    if more:
                        invert(n)
                    if u == 0:
                        fold(0, 1)
                        residual(g, u, 0)
                        scale(0)
                        fold(2)
                        scale(1, 2)
                        split(0)
                        fold(3)
                        residual(g, u, 1)
                        norm(g, u, 0)
                        scale(3)
                        fold(4)
                        scale(4)
                        split(1)
                        scale(5)
                        fold(5)
                        residual(g, u, 2)
                        norm(g, u, 1)
                        scale(6)
                        fold(6)
                        scale(7)
                        split(2, 3)
                        fold(7)
                        if not last:
                            split_ctx(g + 1)
                    elif u == 1:
                        residual(g, u, 0)
                        scale(0, 1, 2)
                        split(0)
                        residual(g, u, 1)
                        norm(g, u, 0)
                        scale(3, 4)
                        split(1)
                        scale(5)
                        residual(g, u, 2)
                        norm(g, u, 1)
                        scale(6, 7)
                        split(2, 3)
                    elif u == 2:
                        residual(g, u, 0)
                        scale(0, 1)
                        if not last:
                            split_v(g + 1)
                        scale(2)
                        split(0)
                        residual(g, u, 1)
                        norm(g, u, 0)
                        scale(3, 4)
                        fold(8)
                        split(1)
                        scale(5)
                        fold(9)
                        residual(g, u, 2)
                        norm(g, u, 1)
                        scale(6, 7)
                        fold(10)
                        split(2)
                        fold(11)
                        split(3)
                    else:
                        fold(12)
                        residual(g, u, 0)
                        scale(0, 1)
                        fold(13)
                        scale(2)
                        split(0)
                        residual(g, u, 1)
                        norm(g, u, 0)
                        scale(3, 4)
                        fold(14)
                        split(1)
                        scale(5)
                        residual(g, u, 2)
                        norm(g, u, 1)
                        scale(6, 7)
                        split(2)
                        fold(15)
                        split(3)
                    residual(g, u, 3)
                    norm(g, u, 2)
                    norm(g, u, 3)

            dve.tensor_scalar(key_max[:, :], least[:, :], -1.0, MASKED, ALU.mult, ALU.add).then_inc(key_max_done, 1)
            dve.wait_ge(key_max_done, 1)
            dve.tensor_tensor(score_max[:, :], score_max[:, :], key_max[:, :], ALU.max).then_inc(max_local, 1)
            dve.wait_ge(max_global, 1)
            dve.tensor_scalar(neg_max[:, :], key_max[:, :], -1.0, None, ALU.mult).then_inc(max_done, 1)
            dve.wait_ge(sum_in, 32)
            split_v(0)
            invert(0)
            for k in range(4):
                split_u(-1, NP + 2 * k)
                scale_p(0, 0, 2 * k)
                split_u(-1, NP + 2 * k + 1)
                scale_p(0, 0, 2 * k + 1)
                split_p(0, 0, k)
            with dve.Fori(0, NG - 1) as g:
                group(g, False)
            group(NG - 1, True)

        @block.gpsimd
        def _(pool):
            pool.wait_ge(max_local, 1)
            pool.partition_all_reduce(key_max[:, :], score_max[:, :], P, bass.bass_isa.ReduceOp.max)\
                .then_inc(max_global, 1)
            pool.memset(minus_half[:, :], -0.5).then_inc(consts_done, 1)
            pool.memset(ln_eps[:, :], LN_EPS).then_inc(consts_done, 1)
            pool.wait_ge(consts_done, 2)
            pool.wait_ge(affine_in, 48)

            def add_bo(g, u):
                s = u % UNITS
                pool.wait_ge(x_in[s], 16 * g + 16 * (u // UNITS) + 16)
                for t in range(TB):
                    y = y32[:, s, t, :]
                    add = pool.tensor_tensor(y, y, bo_b[:, :], ALU.add)
                add.then_inc(bo_added, 1)

            def inv_std(g, u, t):
                k = (g * UNITS + u) * TB + t + 1
                pool.wait_ge(mean_done, k)
                pool.tensor_tensor(var_eps[:, t:t + 1], mean_var[:, t, 1:2], ln_eps[:, :], ALU.add)\
                    .then_inc(eps_added, 1)
                pool.wait_ge(eps_added, k)
                pool.tensor_tensor(rstd[:, t:t + 1], var_eps[:, t:t + 1], minus_half[:, :], ALU.pow)\
                    .then_inc(rstd_done, 1)

            def affine(g, u, t):
                k = (g * UNITS + u) * TB + t + 1
                y = y32[:, u, t, :]
                pool.wait_ge(normed, k)
                pool.tensor_tensor(y, y, gamma_b[:, :], ALU.mult).then_inc(scaled, 1)
                pool.wait_ge(scaled, k)
                pool.tensor_tensor(y, y, beta_b[:, :], ALU.add).then_inc(shifted, 1)

            def group(g, last):
                for u in range(UNITS):
                    if not (last and u == UNITS - 1):
                        add_bo(g, u + 1)
                    inv_std(g, u, 0)
                    for t in range(1, TB):
                        inv_std(g, u, t)
                        affine(g, u, t - 1)
                    affine(g, u, TB - 1)

            add_bo(0, 0)
            with pool.Fori(0, NG - 1) as g:
                group(g, False)
            group(NG - 1, True)


def kernel(**inputs):
    import numpy as np
    import concourse.bacc as bacc
    from concourse.bass_utils import run_bass_kernel_spmd

    a = {k.removeprefix("L0_xattn_"): np.asarray(v) for k, v in inputs.items()}

    def columns(v):
        return v.reshape(-1, P).T

    sel_sum = np.zeros((P, NP // 2, 32), np.float32)
    sel_bc = np.zeros((P, NP, 2, P), np.float32)
    part = np.zeros((P, 2), np.float32)
    for k in range(COPIES):
        for h in range(2):
            for p in range(NP):
                row, keys = 8 * k + 2 * (p % 4) + h, slice(h * NK, (h + 1) * NK)
                sel_sum[keys, p % 4, row] = 1.0
                for th in range(2):
                    q = 2 * th + p // 4
                    sel_bc[32 * q + row, p, th, keys] = P_SCALE
                    part[32 * q + row] = (-1.0 if k >= 1 else 0.0, -1.0 if k >= 2 else 0.0)

    turned = np.roll(np.arange(B), -1)
    context = a["ctx_1024"].transpose(2, 0, 1).reshape(DC, P, B, NK)
    arrays = {
        "xT": a["x"].transpose(0, 2, 1).reshape(B, DC, P, T)[turned],
        "x": a["x"],
        "ctxT": context.reshape(DC, P, B * NK),
        "ctxT_turned": context[:, :, [*turned, *range(GB)]].reshape(DC, P, (B + GB) * NK),
        "maskT": a["mask_BxSxS2_ik1"].transpose(0, 2, 1)[turned],
        "wk": a["Wk"].reshape(DC, P, HD),
        "wqT": a["Wq"].T.reshape(4, 2, P, D).transpose(0, 2, 1, 3).reshape(4, P, 2 * D),
        "wv": a["Wv"].reshape(DC, P, HD),
        "wo": a["Wo"].reshape(4, 2, P, D).transpose(0, 2, 1, 3).reshape(4, P, 2 * D),
        "bk": columns(a["bk"]), "bq": columns(a["bq"]), "bv": columns(a["bv"]),
        "bo": a["bo"], "gamma": a["gamma"], "beta": a["beta"],
        "sel_sum": sel_sum, "sel_bc": sel_bc.reshape(P, 2, -1).transpose(1, 0, 2), "part": part,
    }
    nc = bacc.Bacc("TRN2", target_bir_lowering=False, num_devices=1)
    aps = {}
    for name, v in arrays.items():
        arrays[name] = v = np.ascontiguousarray(v)
        aps[name] = nc.dram_tensor(name + "_in", v.shape, mybir.dt.from_np(v.dtype), kind="ExternalInput").ap()
    out = nc.dram_tensor("out", (B, T, D), F32, kind="ExternalOutput").ap()
    build(nc, *(aps[k] for k in ("xT", "x", "ctxT", "ctxT_turned", "maskT", "wk", "wqT", "wv", "wo", "bk", "bq", "bv",
                                 "bo", "gamma", "beta", "sel_sum", "sel_bc", "part")), out)
    r = run_bass_kernel_spmd(nc, [{name + "_in": v for name, v in arrays.items()}], core_ids=[0])
    return r.results[0]["out"]
```

```python
from contextlib import ExitStack

import concourse.bass as bass
from concourse import mybir

F32 = mybir.dt.float32
F16 = mybir.dt.float16
BF16 = mybir.dt.bfloat16
I32 = mybir.dt.int32
ALU = mybir.AluOpType
ACT = mybir.ActivationFunctionType
AX = mybir.AxisListType

P = 128
B, T, D = 16, 1024, 512
H, DK, NK = 16, 64, 64
HD = H * DK
DC = D // P
NP = HD // P
GB = 2
NG = B // GB
TT = 512
UB = T // TT
UNITS = GB * UB
NU = B * UB
TB = TT // P
KC = GB * NK
GT = NP * DC // 2
SBANKS, GBANKS = 2, 4
EARLY = NP // 2

W_SCALE, CTX_SCALE, X_SCALE = 64.0, 4.0, 4.0
K_SCALE, G_SCALE = 8.0, 16.0
V_SCALE, U_SCALE, P_SCALE = 32.0, 64.0, 1024.0
MASKED = -1.0e30
TINY, LN_EPS = 1e-15, 1e-5

COPIES = 3


def build(nc, xT, x, ctxT, ctxT_turned, maskT, wk, wqT, wv, wo, bk, bq, bv, bo, gamma, beta,
          sel_sum_d, sel_bc_d, part_d, out):
    scores_d = nc.dram_tensor("scores", (NU - UB, P, NP * TT), F32, kind="Internal").ap()

    with ExitStack() as ctx:
        def sb(name, shape, dt=F32, scope=ctx):
            return scope.enter_context(nc.sbuf_tensor(name, shape, dt))

        wk_hi, wk_lo = sb("wk_hi", [P, DC, HD], F16), sb("wk_lo", [P, DC, HD], F16)
        u0_hi, u0_lo = (w[:, :, :].rearrange("r c n -> r (c n)") for w in (wk_hi, wk_lo))
        wv_hi, wv_lo = sb("wv_hi", [P, DC, HD], F16), sb("wv_lo", [P, DC, HD], F16)
        wo2 = sb("wo2", [P, NP, 2, D], F16)
        bkv = sb("bkv", [P, 2, NP])
        ctx32 = sb("ctx32", [P, DC, KC])
        ctx_hi, ctx_lo = sb("ctx_hi", [P, DC, KC], F16), sb("ctx_lo", [P, DC, KC], F16)
        kv32 = sb("kv32", [P, NP, KC])
        kv_hi, kv_lo = sb("kv_hi", [P, NP, GB, 2, NK], F16), sb("kv_lo", [P, NP, GB, 2, NK], F16)
        s32 = sb("s32", [P, 2, NP, TT])
        sel_sum, sel_bc = sb("sel_sum", [P, NP // 2, 32]), sb("sel_bc", [P, NP, 2, P], BF16)
        least = sb("least", [P, 1])
        score_max, key_max, neg_max = sb("score_max", [P, 1]), sb("key_max", [P, 1]), sb("neg_max", [P, 1])

        scores_phase(nc, xT, ctxT_turned, maskT, wk, wqT, wv, wo, bk, bq, bv, sel_bc_d, scores_d,
                     wk_hi, wk_lo, wv_hi, wv_lo, wo2, u0_hi, u0_lo, bkv, ctx32, ctx_hi, ctx_lo,
                     kv32, kv_hi, kv_lo, s32, sel_bc, score_max, least)
        output_phase(nc, x, ctxT, scores_d, bo, gamma, beta, sel_sum_d, part_d, out,
                     wv_hi, wv_lo, wo2, u0_hi, u0_lo, bkv, ctx32, ctx_hi, ctx_lo,
                     kv32, kv_hi, kv_lo, s32, sel_sum, sel_bc, score_max, least, key_max, neg_max)


def split_product(pe, out, lhs, rhs, first, last):
    (lhs_hi, lhs_lo), (rhs_hi, rhs_lo) = lhs, rhs
    pe.matmul(out, lhs_hi, rhs_hi, start=first, stop=False)
    pe.matmul(out, lhs_hi, rhs_lo, start=False, stop=False)
    return pe.matmul(out, lhs_lo, rhs_hi, start=False, stop=last)


def project_heads(pe, banks, w_hi, w_lo, ctx_hi, ctx_lo, ready, pairs=range(NP)):
    for p in pairs:
        o = banks[p // 4][:, (p % 4) * KC:(p % 4 + 1) * KC]
        cols = slice(p * P, (p + 1) * P)
        for c in range(DC):
            mm = split_product(pe, o, (w_hi[:, c, cols], w_lo[:, c, cols]),
                               (ctx_hi[:, c, :], ctx_lo[:, c, :]), c == 0, c == DC - 1)
        if p % 4 == 3:
            mm.then_inc(ready, 1)


def rows_of(h):
    return slice(h * DK, (h + 1) * DK)


def of_head(kv, h, rows):
    return kv[rows_of(rows), :, :, h, :].rearrange("r p b k -> r (p b) k")


def projected(kv32, h):
    return kv32[rows_of(h), :, :].rearrange("r p (b k) -> r (p b) k", b=GB)


def round_heads(act, kv_hi, kv32, scale, done):
    for other in range(2):
        for h in range(2):
            rows = 1 - h if other else h
            act.activation(of_head(kv_hi, h, rows), projected(kv32, h), ACT.Copy, scale=scale).then_inc(done, 1)


def split_heads(dve, kv_lo, kv_hi, kv32, scale, done):
    for h in range(2):
        dve.scalar_tensor_tensor(of_head(kv_lo, h, h), projected(kv32, h), scale, of_head(kv_hi, h, h),
                                 ALU.mult, ALU.subtract).then_inc(done, 1)


def fold_head_outputs(pe, bank, kv_hi, kv_lo, wo2, p, b):
    for k, half in enumerate((kv_hi, kv_lo)):
        for h in range(2):
            mm = pe.matmul(bank[rows_of(h), :], half[:, p, b, h, :], wo2[:, p, h, :],
                           start=(k == 0), stop=(k == 1), skip_group_check=True)
    return mm


def scores_phase(nc, xT, ctxT, maskT, wk, wqT, wv, wo, bk, bq, bv, sel_bc_d, scores_d,
                 wk_hi, wk_lo, wv_hi, wv_lo, wo2, u0_hi, u0_lo, bkv, ctx32, ctx_hi, ctx_lo,
                 kv32, kv_hi, kv_lo, s32, sel_bc, score_max, least):
    with ExitStack() as ctx:
        def sb(name, shape, dt=F32):
            return ctx.enter_context(nc.sbuf_tensor(name, shape, dt))

        def sem(name):
            return ctx.enter_context(nc.semaphore(name))

        def bank(name):
            return ctx.enter_context(nc.psum_tensor(name, [P, 512], F32))

        wq2 = sb("wq2", [P, NP, 2, D], F16)
        w32 = sb("w32", [P, 2, 1024])
        bq32, bq2 = sb("bq32", [P, NP]), sb("bq2", [P, NP, 2], F16)
        x32 = sb("x32", [P, 2, DC, TT])
        x_hi, x_lo = sb("x_hi", [P, 2, DC, TT], F16), sb("x_lo", [P, 2, DC, TT], F16)
        g_hi, g_lo = sb("g_hi", [P, NP, DC, GB, P], F16), sb("g_lo", [P, NP, DC, GB, P], F16)
        c_bias = sb("c_bias", [P, NP * GB])
        mask32, mask_add = sb("mask32", [P, T], I32), sb("mask_add", [P, 2, T])
        tile_max, mask_min = sb("tile_max", [P, 2]), sb("mask_min", [P, 1])

        ps_s = [bank(f"ps_s{i}") for i in range(SBANKS)]
        ps_g = [bank(f"ps_g{i}") for i in range(GBANKS)]
        ps_k = [bank(f"ps_k{i}") for i in range(2)]

        w_in = [sem(f"w_in{i}") for i in range(8)]
        w_hi_done, w_lo_done = sem("w_hi_done"), sem("w_lo_done")
        small_in, bq_done = sem("small_in"), sem("bq_done")
        ctx_in, ctx_hi_done, ctx_lo_done = sem("ctx_in"), sem("ctx_hi_done"), sem("ctx_lo_done")
        x_in = [sem(f"x_in{i}") for i in range(2)]
        x_hi_done, x_lo_done = sem("x_hi_done"), sem("x_lo_done")
        mask_in, mask_ready = sem("mask_in"), sem("mask_ready")
        zeroed = sem("zeroed")
        k_summed, k32_done = sem("k_summed"), sem("k32_done")
        k_hi_done, k_lo_done = sem("k_hi_done"), sem("k_lo_done")
        c_summed, c_ready = sem("c_summed"), sem("c_ready")
        g_summed, g_hi_done, g_lo_done = sem("g_summed"), sem("g_hi_done"), sem("g_lo_done")
        s_summed, s_out, s_masked = sem("s_summed"), sem("s_out"), sem("s_masked")
        least_steps, max_steps = sem("least_steps"), sem("max_steps")
        s_stored = [sem(f"s_stored{i}") for i in range(2)]
        weights = (wk, wqT, wv, wo)

        def chunk(i):
            return weights[i // 4][i % 4]

        def weight_parts(i):
            c, w32_i = i % 4, staging(i)
            if i // 4 in (0, 2):
                hi, lo = (wk_hi, wk_lo) if i < 4 else (wv_hi, wv_lo)
                yield hi[:, c, :], lo[:, c, :], w32_i
            else:
                w2 = wq2 if i < 8 else wo2
                for h in range(2):
                    yield (*(w2[rows_of(rows), 2 * c:2 * c + 2, h, :] for rows in (h, 1 - h)),
                           w32_i[rows_of(h), :].rearrange("r (p d) -> r p d", p=2))

        def staging(i):
            if i < 8:
                return s32[:, i // 4, 2 * (i % 4):2 * (i % 4) + 2, :].rearrange("r p t -> r (p t)")
            return w32[:, i % 2, :]

        def w_loaded(i):
            return w_in[i % 8 if i < 8 else i % 2], 16 if i < 8 else 16 * ((i - 8) // 2 + 2)

        block = ctx.enter_context(nc.Block())

        @block.sync
        def _(sp):
            def load_weight(i):
                if i >= 10:
                    sp.wait_ge(w_lo_done, i - 1)
                sp.dma_start(staging(i), chunk(i)).then_inc(w_loaded(i)[0], 16)

            def load_sel():
                sp.wait_ge(w_lo_done, 16)
                for i in range(2):
                    sp.dma_start(w32[:, i, :], sel_bc_d[i]).then_inc(w_loaded(16 + i)[0], 16)

            def load_ctx(g):
                sp.dma_start(ctx32[:, :, :], ctxT[:, :, bass.ds(g * KC, KC)].rearrange("c p k -> p c k"))\
                  .then_inc(ctx_in, 16)

            def load_x(n, b, u):
                sp.wait_ge(x_lo_done, n + 1)
                sp.dma_start(x32[:, u % 2, :, :],
                             xT[bass.ds(b, 1), :, :, (u % 2) * TT:(u % 2 + 1) * TT]
                             .rearrange("a c p t -> p (a c) t")).then_inc(x_in[u % 2], 16)

            def load_mask(b):
                sp.wait_ge(mask_ready, b + 1)
                for h in range(2):
                    sp.dma_start(mask32[h * NK:(h + 1) * NK, :],
                                 maskT[bass.ds(b, 1), :, :].rearrange("a k t -> (a k) t")).then_inc(mask_in, 16)

            def store_scores(n, u):
                sp.wait_ge(s_masked, (n + 2) * NP)
                sp.dma_start(scores_d[bass.ds(n, 1), :, :].rearrange("a p n -> p (a n)"),
                             s32[:, u % 2, :, :].rearrange("r p t -> r (p t)")).then_inc(s_stored[u % 2], 16)

            for i in range(2):
                sp.sem_inc(s_stored[i], 16)
            load_ctx(0)
            for half, w in enumerate((bk, bv)):
                sp.dma_start(bkv[:, half, :], w).then_inc(small_in, 16)
            sp.dma_start(bq32[:, :], bq).then_inc(small_in, 16)
            for i in range(8):
                load_weight(i)
            load_x(0, 0, 0)
            load_mask(0)
            load_x(1, 0, 1)

            def group(g, last):
                if last:
                    load_weight(8)
                    load_weight(9)
                load_mask(g * GB + 1)
                sp.wait_ge(ctx_lo_done, g + 1)
                load_ctx(g + 1)
                for u in range(UNITS):
                    if not (last and u >= UNITS - 2):
                        load_x(g * UNITS + u + 2, g * GB + (u + 2) // UB, u)
                    if u == 2 and not last:
                        load_mask(g * GB + 2)
                    if last and u < UB:
                        for i in range(10, 14) if u == 0 else range(14, 16):
                            load_weight(i)
                    if last and u == 2:
                        load_sel()
                    if not (last and u >= UNITS - UB):
                        store_scores(g * UNITS + u, u)

            with sp.Fori(0, NG - 1) as g:
                group(g, False)
            group(NG - 1, True)
            for i in range(2):
                sp.wait_ge(s_stored[i], 16 + 16 * (NU // 2 - 1))

        @block.tensor
        def _(pe):
            pe.sem_inc(s_summed, 2 * NP)

            def project(g, w_hi, w_lo):
                pe.wait_ge(ctx_lo_done, g + 1)
                pe.wait_ge(c_ready, g + 1)
                project_heads(pe, ps_k, w_hi, w_lo, ctx_hi, ctx_lo, k_summed)

            def bias(g, pairs):
                for p in pairs:
                    for b in range(GB):
                        o = ps_k[0][:, 2 * (GB * p + b):2 * (GB * p + b) + 2]
                        for k, half in enumerate((kv_hi, kv_lo)):
                            mm = pe.matmul(o, half[:, p, b, :, :].rearrange("r h k -> r (h k)"), bq2[:, p, :],
                                           start=(k == 0), stop=(k == 1))
                if p == NP - 1:
                    mm.then_inc(c_summed, 1)

            def fold_q(g, p):
                if p == 0:
                    pe.wait_ge(k_hi_done, 4 * g + 4)
                    pe.wait_ge(k_lo_done, 2 * g + 2)
                for i in (2 * p, 2 * p + 1):
                    dp = i % 2
                    pe.wait_ge(g_lo_done, g * GT + i + 1)
                    tile = ps_g[i % GBANKS][:, :].rearrange("r (j b h k) -> r j b h k", j=2, b=GB, h=2)
                    for j in range(2):
                        cols = slice((2 * dp + j) * P, (2 * dp + j + 1) * P)
                        for h in range(2):
                            for k, half in enumerate((kv_hi, kv_lo)):
                                mm = pe.matmul(tile[:, j, :, h, :], wq2[:, p, h, cols], half[:, p, :, h, :],
                                               start=(k == 0), stop=(k == 1))
                    mm.then_inc(g_summed, 1)

            def fold_o(p):
                if p == 0:
                    pe.wait_ge(k_hi_done, 4 * NG + 4)
                    pe.wait_ge(k_lo_done, 2 * NG + 2)
                pe.wait_ge(g_lo_done, NG * GT + p + 1)
                fold_head_outputs(pe, ps_g[p % GBANKS], kv_hi, kv_lo, wo2, p, 0).then_inc(g_summed, 1)

            def scores(g, u, with_u):
                n, b = g * UNITS + u, u // UB
                pe.wait_ge(x_lo_done, n + 3)
                for p in range(NP):
                    if u == 0 and p < NP - EARLY:
                        fold_q(g, EARLY + p)
                    if u == 0:
                        pe.wait_ge(g_lo_done, g * GT + 2 * p + 2 + GBANKS)
                    pe.wait_ge(s_out, n * NP + p + 1)
                    for c in range(DC):
                        mm = split_product(pe, ps_s[p % SBANKS][:, :],
                                           (g_hi[:, p, c, b, :], g_lo[:, p, c, b, :]),
                                           (x_hi[:, u % 2, c, :], x_lo[:, u % 2, c, :]), c == 0, c == DC - 1)
                    mm.then_inc(s_summed, 1)
                    if with_u and p > 0:
                        fold_o(p - 1)
                if with_u:
                    fold_o(NP - 1)

            def group(g, last):
                for p in range(EARLY):
                    fold_q(g, p)
                    bias(g, (2 * p, 2 * p + 1))
                for u in range(UNITS):
                    scores(g, u, last and u == UNITS - 1)
                    if u == UNITS - 2:
                        project(g + 1, *((wv_hi, wv_lo) if last else (wk_hi, wk_lo)))

            pe.wait_ge(w_lo_done, 4)
            pe.wait_ge(zeroed, 1)
            project(0, wk_hi, wk_lo)
            pe.wait_ge(w_lo_done, 8)
            pe.wait_ge(bq_done, 4)
            with pe.Fori(0, NG - 1) as g:
                group(g, False)
            group(NG - 1, True)

        @block.scalar
        def _(act):
            act.sem_inc(s_out, SBANKS)

            def split_weight(i):
                act.wait_ge(*w_loaded(i))
                for hi, _, w in weight_parts(i):
                    rounded = act.activation(hi, w, ACT.Copy, scale=W_SCALE)
                rounded.then_inc(w_hi_done, 1)

            def split_ctx(g):
                act.wait_ge(ctx_in, 16 * (g + 1))
                act.activation(ctx_hi[:, :, :], ctx32[:, :, :], ACT.Copy, scale=CTX_SCALE).then_inc(ctx_hi_done, 1)

            def round_x(g, u):
                act.wait_ge(x_in[u % 2], g * (8 * UNITS) + 16 * (u // 2 + 1))
                act.wait_ge(s_summed, (g * UNITS + u + 1) * NP)
                act.activation(x_hi[:, u % 2, :, :], x32[:, u % 2, :, :], ACT.Copy, scale=X_SCALE)\
                   .then_inc(x_hi_done, 1)

            def round_k(g, half=0, scale=K_SCALE):
                if not (isinstance(g, int) and g == 0):
                    act.wait_ge(k_lo_done, 2 * g)
                for p in range(NP):
                    if p % 4 == 0:
                        act.wait_ge(k_summed, 2 * g + p // 4 + 1)
                    act.activation(kv32[:, p, :], ps_k[p // 4][:, (p % 4) * KC:(p % 4 + 1) * KC], ACT.Identity,
                                   bias=bkv[:, half, p:p + 1], scale=1 / (W_SCALE * CTX_SCALE)).then_inc(k32_done, 1)
                act.wait_ge(k32_done, NP * (g + 1))
                round_heads(act, kv_hi, kv32, scale, k_hi_done)

            def round_g(g, p):
                if p == 0:
                    act.wait_ge(s_summed, (g * UNITS + 2) * NP)
                for i in (2 * p, 2 * p + 1):
                    dp = i % 2
                    act.wait_ge(g_summed, g * GT + i + 1)
                    act.activation(g_hi[:, p, 2 * dp:2 * dp + 2, :, :].rearrange("r c b k -> r (c b k)"),
                                   ps_g[i % GBANKS][:, :], ACT.Copy, scale=G_SCALE / (W_SCALE * K_SCALE))\
                       .then_inc(g_hi_done, 1)

            def round_u(p):
                act.wait_ge(g_summed, NG * GT + p + 1)
                act.activation(u0_hi[:, p * D:(p + 1) * D], ps_g[p % GBANKS][:, :], ACT.Copy,
                               scale=U_SCALE / (W_SCALE * V_SCALE)).then_inc(g_hi_done, 1)

            def copy_sel(i):
                act.wait_ge(*w_loaded(16 + i))
                act.activation(sel_bc[:, 4 * i:4 * i + 4, :, :].rearrange("r p t k -> r (p t k)"),
                               w32[:, i, :], ACT.Copy)

            def scores_out(g, u, last):
                n = g * UNITS + u
                act.wait_ge(s_stored[u % 2], g * (8 * UNITS) + 16 * (u // 2 + 1))
                if u == 0:
                    act.wait_ge(c_ready, g + 2)
                for p in range(NP):
                    if u == 0 and p < NP - EARLY:
                        round_g(g, EARLY + p)
                    act.wait_ge(s_summed, n * NP + p + 1 + 2 * NP)
                    k = GB * p + u // UB
                    act.activation(s32[:, u % 2, p, :], ps_s[p % SBANKS][:, :], ACT.Identity, bias=c_bias[:, k:k + 1],
                                   scale=1 / (G_SCALE * X_SCALE)).then_inc(s_out, 1)
                    if p == NP // 2 and not (last and u == UNITS - 1):
                        round_x(g, u + 1)
                    if last and u < 2 and p % 2 == 1:
                        split_weight(8 + 4 * u + p // 2)
                    if last and u == UNITS - 1:
                        if p > 0:
                            round_u(p - 1)
                        if p in (3, 5):
                            copy_sel(p // 4)
                if last and u == UNITS - 1:
                    round_u(NP - 1)

            def group(g, last):
                for p in range(EARLY):
                    round_g(g, p)
                for u in range(UNITS):
                    scores_out(g, u, last)
                    if u == 1:
                        act.wait_ge(k_summed, 2 * g + 2)
                        split_ctx(g + 1)
                    if u == UNITS - 2:
                        act.wait_ge(g_summed, (g + 1) * GT)
                        if last:
                            round_k(g + 1, half=1, scale=V_SCALE)
                        else:
                            round_k(g + 1)

            split_ctx(0)
            act.wait_ge(small_in, 48)
            for h in range(2):
                act.activation(bq2[rows_of(h), :, h], bq32[rows_of(h), :], ACT.Copy, scale=W_SCALE)\
                   .then_inc(bq_done, 1)
            for i in range(8):
                split_weight(i)
            round_k(0)
            round_x(0, 0)
            with act.Fori(0, NG - 1) as g:
                group(g, False)
            group(NG - 1, True)

        @block.vector
        def _(dve):
            dve.sem_inc(x_lo_done, 2)
            dve.sem_inc(mask_ready, 1)
            dve.sem_inc(g_lo_done, GBANKS)
            dve.sem_inc(s_masked, NP)
            dve.sem_inc(c_ready, 1)
            dve.memset(kv_lo[:, :, :, :, :], 0.0).then_inc(zeroed, 1)
            dve.memset(score_max[:, :], MASKED).then_inc(max_steps, 1)
            dve.memset(tile_max[:, :], MASKED).then_inc(max_steps, 1)
            dve.memset(least[:, :], 0.0).then_inc(least_steps, 1)
            dve.wait_ge(least_steps, 1)

            def split_weight(i):
                dve.wait_ge(w_hi_done, i + 1)
                for hi, lo, w in weight_parts(i):
                    split = dve.scalar_tensor_tensor(lo, w, W_SCALE, hi, ALU.mult, ALU.subtract)
                split.then_inc(w_lo_done, 1)

            def split_ctx(g):
                dve.wait_ge(ctx_hi_done, g + 1)
                dve.scalar_tensor_tensor(ctx_lo[:, :, :], ctx32[:, :, :], CTX_SCALE, ctx_hi[:, :, :],
                                         ALU.mult, ALU.subtract).then_inc(ctx_lo_done, 1)

            def split_x(g, u):
                dve.wait_ge(x_hi_done, g * UNITS + u + 1)
                dve.scalar_tensor_tensor(x_lo[:, u % 2, :, :], x32[:, u % 2, :, :], X_SCALE, x_hi[:, u % 2, :, :],
                                         ALU.mult, ALU.subtract).then_inc(x_lo_done, 1)

            def split_k(g, scale=K_SCALE):
                dve.wait_ge(k_hi_done, 4 * g + 2)
                split_heads(dve, kv_lo, kv_hi, kv32, scale, k_lo_done)

            def split_g(g, p):
                for i in (2 * p, 2 * p + 1):
                    dp = i % 2
                    at = lambda a: a[:, p, 2 * dp:2 * dp + 2, :, :].rearrange("r c b k -> r (c b k)")
                    dve.wait_ge(g_hi_done, g * GT + i + 1)
                    dve.scalar_tensor_tensor(at(g_lo), ps_g[i % GBANKS][:, :], G_SCALE / (W_SCALE * K_SCALE), at(g_hi),
                                             ALU.mult, ALU.subtract).then_inc(g_lo_done, 1)

            def bias(g):
                dve.wait_ge(c_summed, g + 1)
                dve.wait_ge(s_out, g * UNITS * NP + SBANKS)
                for h in range(2):
                    c = ps_k[0][rows_of(h), 0:2 * NP * GB].rearrange("r (n h) -> r n h", h=2)[:, :, h]
                    scaled = dve.tensor_scalar(c_bias[rows_of(h), :], c, 1 / (W_SCALE * K_SCALE), None, ALU.mult)
                scaled.then_inc(c_ready, 1)

            def mask(g, j):
                b = g * GB + j
                dve.wait_ge(mask_in, 32 * (b + 1))
                dve.tensor_scalar(mask_add[:, j % GB, :], mask32[:, :], -MASKED, MASKED, ALU.mult, ALU.add)\
                   .then_inc(mask_ready, 1)
                dve.wait_ge(mask_ready, b + 2)
                dve.tensor_reduce(mask_min[:, :], mask_add[:, j % GB, :], axis=AX.X, op=ALU.min)\
                   .then_inc(least_steps, 1)
                dve.wait_ge(least_steps, 2 * b + 2)
                dve.tensor_tensor(least[:, :], least[:, :], mask_min[:, :], ALU.min).then_inc(least_steps, 1)

            def raise_max(k, p):
                dve.wait_ge(s_masked, k + NP)
                dve.wait_ge(max_steps, k + 2)
                dve.tensor_tensor(score_max[:, :], score_max[:, :], tile_max[:, (p + 1) % 2:(p + 1) % 2 + 1],
                                  ALU.max).then_inc(max_steps, 1)

            def split_u(p):
                dve.wait_ge(g_hi_done, NG * GT + p + 1)
                at = slice(p * D, (p + 1) * D)
                dve.scalar_tensor_tensor(u0_lo[:, at], ps_g[p % GBANKS][:, :], U_SCALE / (W_SCALE * V_SCALE),
                                         u0_hi[:, at], ALU.mult, ALU.subtract).then_inc(g_lo_done, 1)

            def mask_scores(g, u, last):
                n, j, t0 = g * UNITS + u, u // UB, (u % UB) * TT
                for p in range(NP):
                    if u == 0 and p < NP - EARLY:
                        split_g(g, EARLY + p)
                    dve.wait_ge(s_out, n * NP + p + 1 + SBANKS)
                    raise_max(n * NP + p, p)
                    dve.tensor_tensor_reduce(s32[:, u % 2, p, :], s32[:, u % 2, p, :], mask_add[:, j, t0:t0 + TT],
                                             1.0, MASKED, ALU.add, ALU.max, tile_max[:, p % 2:p % 2 + 1])\
                       .then_inc(s_masked, 1)
                    if last and u < 2 and p % 2 == 1:
                        split_weight(8 + 4 * u + p // 2)
                    if last and u == UNITS - 1 and p > 0:
                        split_u(p - 1)
                    if p == NP // 2 and not (last and u == UNITS - 1):
                        split_x(g, u + 1)
                    if p == NP // 2 + 1 and u % UB == 1 and not (last and u == UNITS - 1):
                        mask(g, (u + 1) // UB)
                if last and u == UNITS - 1:
                    split_u(NP - 1)

            def group(g, last):
                for p in range(EARLY):
                    split_g(g, p)
                bias(g)
                for u in range(UNITS):
                    mask_scores(g, u, last)
                    if u == 1:
                        split_ctx(g + 1)
                    if u == UNITS - 2:
                        split_k(g + 1, V_SCALE if last else K_SCALE)

            split_ctx(0)
            dve.wait_ge(bq_done, 2)
            for h in range(2):
                dve.scalar_tensor_tensor(bq2[rows_of(1 - h), :, h], bq32[rows_of(h), :], W_SCALE,
                                         bq2[rows_of(h), :, h], ALU.mult, ALU.subtract).then_inc(bq_done, 1)
            dve.wait_ge(zeroed, 1)
            for i in range(8):
                split_weight(i)
            split_k(0)
            split_x(0, 0)
            mask(0, 0)
            with dve.Fori(0, NG - 1) as g:
                group(g, False)
            group(NG - 1, True)

            raise_max(NU * NP, NP)


def output_phase(nc, x, ctxT, scores_d, bo, gamma, beta, sel_sum_d, part_d, out,
                 wv_hi, wv_lo, wo2, u0_hi, u0_lo, bkv, ctx32, ctx_hi, ctx_lo,
                 kv32, kv_hi, kv_lo, s32, sel_sum, sel_bc, score_max, least, key_max, neg_max):
    HT = TT // 2

    with ExitStack() as ctx:
        def sb(name, shape, dt=F32):
            return ctx.enter_context(nc.sbuf_tensor(name, shape, dt))

        def sem(name):
            return ctx.enter_context(nc.semaphore(name))

        def bank(name):
            return ctx.enter_context(nc.psum_tensor(name, [P, 512], F32))

        u1_hi, u1_lo = sb("u1_hi", [P, NP * D], F16), sb("u1_lo", [P, NP * D], F16)
        p_hi, p_lo = sb("p_hi", [P, 2, NP, TT], F16), sb("p_lo", [P, 2, NP, TT], F16)
        y32 = sb("y32", [P, UNITS, TB, D])
        gamma_b, beta_b, bo_b = sb("gamma_b", [P, D]), sb("beta_b", [P, D]), sb("bo_b", [P, D])
        part = sb("part", [P, 2])
        den, r32, rest = sb("den", [P, HT]), sb("r32", [P, HT]), sb("rest", [P, HT])
        r_hi, r_mid, r_all = sb("r_hi", [P, HT], BF16), sb("r_mid", [P, HT], BF16), sb("r_all", [P, HT], BF16)
        stats, mean_var = sb("stats", [P, TB, 6]), sb("mean_var", [P, TB, 2])
        var_eps, rstd, minus_half = sb("var_eps", [P, TB]), sb("rstd", [P, TB]), sb("minus_half", [P, 1])
        ln_eps = sb("ln_eps", [P, 1])

        ps_sum = bank("ps_sum")
        ps_bc = [bank(f"ps_bc{i}") for i in range(2)]
        ps_o = [bank(f"ps_o{i}") for i in range(2)]
        ps_u = [bank(f"ps_u{i}") for i in range(2)]

        sum_in, affine_in, consts_done = sem("sum_in"), sem("affine_in"), sem("consts_done")
        key_max_done, max_local, max_global, max_done = (sem(n) for n in (
            "key_max_done", "max_local", "max_global", "max_done"))
        ctx_in, ctx_hi_done, ctx_lo_done = sem("ctx2_in"), sem("ctx2_hi_done"), sem("ctx2_lo_done")
        s_in = [sem(f"s_in{i}") for i in range(2)]
        x_in = [sem(f"xres_in{i}") for i in range(UNITS)]
        v_summed, v32_done = sem("v_summed"), sem("v32_done")
        v_hi_done, v_lo_done = sem("v_hi_done"), sem("v_lo_done")
        u_summed, u_hi_done, u_lo_done = sem("u_summed"), sem("u_hi_done"), sem("u_lo_done")
        exp_done, e_summed = sem("exp_done"), sem("e_summed")
        den_done, r_done, r_hi_done = sem("den_done"), sem("r_done"), sem("r_hi_done")
        rest_done, r_mid_done, r_all_done = sem("rest_done"), sem("r_mid_done"), sem("r_all_done")
        r_spread, p_scaled = sem("r_spread"), sem("p_scaled")
        p_hi_done, p_lo_done = sem("p_hi_done"), sem("p_lo_done")
        o_summed, y_added, mean_done = sem("o_summed"), sem("y_added"), sem("mean_done")
        eps_added, rstd_done = sem("eps_added"), sem("rstd_done")
        normed, scaled, shifted, bo_added = sem("normed"), sem("scaled"), sem("shifted"), sem("bo_added")
        y_stored = [sem(f"y_stored{i}") for i in range(UNITS)]

        def tokens(a, b, u):
            t0 = (u % UB) * TT
            return a[bass.ds(b, 1), t0:t0 + TT, :].rearrange("a (n p) d -> p (a n) d", p=P)

        def u_tile(g, j):
            return g * (2 * NP) + NP + j, 1 - j // NP, j % NP

        def u_of(b, p):
            return tuple(u[:, p * D:(p + 1) * D] for u in ((u0_hi, u0_lo), (u1_hi, u1_lo))[b])

        block = ctx.enter_context(nc.Block())

        @block.sync
        def _(sp):
            def load_scores(n, u):
                sp.wait_ge(p_lo_done, 4 * n + 4)
                sp.dma_start(s32[:, u % 2, :, :].rearrange("r p t -> r (p t)"),
                             scores_d[bass.ds(n - UB, 1), :, :].rearrange("a p n -> p (a n)"))\
                  .then_inc(s_in[u % 2], 16)

            def load_x(g, u):
                s = u % UNITS
                sp.wait_ge(y_stored[s], 16 * g + 16 * (u // UNITS) + 16)
                sp.dma_start(y32[:, s, :, :], tokens(x, g * GB + u // UB, u)).then_inc(x_in[s], 16)

            def load_ctx(g):
                sp.dma_start(ctx32[:, :, :], ctxT[:, :, bass.ds(g * KC, KC)].rearrange("c p k -> p c k"))\
                  .then_inc(ctx_in, 16)

            def store_y(g, u):
                sp.wait_ge(shifted, (g * UNITS + u + 1) * TB)
                sp.dma_start(tokens(out, g * GB + u // UB, u % UNITS), y32[:, u % UNITS, :, :])\
                  .then_inc(y_stored[u % UNITS], 16)

            for i in range(UNITS):
                sp.sem_inc(y_stored[i], 16)
            sp.dma_start(sel_sum[:, :, :], sel_sum_d).then_inc(sum_in, 16)
            sp.dma_start(part[:, :], part_d).then_inc(sum_in, 16)
            for to, of in ((gamma_b, gamma), (beta_b, beta), (bo_b, bo)):
                sp.dma_start(to[:, :], of.rearrange("(a d) -> a d", a=1).to_broadcast([P, D])).then_inc(affine_in, 16)
            load_x(0, 0)
            load_x(0, 1)

            def group(g, first, last):
                if not last:
                    sp.wait_ge(ctx_lo_done, g + 1)
                    load_ctx(g + 1)
                for u in range(UNITS):
                    if not (last and u >= UNITS - 2):
                        load_scores(g * UNITS + u + 2, u)
                        load_x(g, u + 2)
                    if not (first and u == 0):
                        store_y(g, u - 1)

            group(0, True, False)
            with sp.Fori(1, NG - 1) as g:
                group(g, False, False)
            group(NG - 1, False, True)
            for t in range(TB):
                sp.wait_ge(shifted, NU * TB - TB + t + 1)
                sp.dma_start(tokens(out, B - 1, UNITS - 1)[:, t, :], y32[:, UNITS - 1, t, :])\
                  .then_inc(y_stored[UNITS - 1], 16)
            for i in range(UNITS - 1):
                sp.wait_ge(y_stored[i], 16 + 16 * NG)
            sp.wait_ge(y_stored[UNITS - 1], 16 + 16 * (NG - 1 + TB))

        @block.tensor
        def _(pe):
            pe.sem_inc(o_summed, 2 * TB)
            pe.sem_inc(v_summed, 2)
            pe.sem_inc(u_summed, NP)

            def fold_o(g, j):
                k, b, p = u_tile(g, j)
                if j % NP == 0:
                    group_of_v = g + 1 if j else g
                    pe.wait_ge(v_hi_done, 4 * group_of_v + 4)
                    pe.wait_ge(v_lo_done, 2 * group_of_v + 2)
                pe.wait_ge(u_lo_done, k + 1)
                fold_head_outputs(pe, ps_u[p % 2], kv_hi, kv_lo, wo2, p, b).then_inc(u_summed, 1)

            def sums(n, s):
                pe.wait_ge(den_done, n + 1)
                for i in range(4):
                    if i % 2 == 0:
                        pe.wait_ge(exp_done, 2 * n + i // 2 + 1)
                    for q in range(4):
                        th, p = q // 2, 4 * (q % 2) + i
                        mm = pe.matmul(ps_sum[32 * q:32 * q + 32, 0:HT], sel_sum[:, i, :],
                                       s32[:, s, p, th * HT:(th + 1) * HT],
                                       start=(i == 0), stop=(i == 3), skip_group_check=True)
                mm.then_inc(e_summed, 1)

            def spread(n, p):
                if p == 0:
                    pe.wait_ge(r_all_done, n + 1)
                pe.wait_ge(p_scaled, n * NP + p + 1)
                for th in range(2):
                    mm = pe.matmul(ps_bc[p % 2][:, th * HT:(th + 1) * HT], sel_bc[:, p, th, :], r_all[:, :],
                                   start=True, stop=True)
                mm.then_inc(r_spread, 1)

            def project(g, pairs):
                if pairs[0] == 0:
                    pe.wait_ge(u_lo_done, (g - 1) * (2 * NP) + 2 * NP + 2)
                    pe.wait_ge(ctx_lo_done, g + 1)
                project_heads(pe, ps_u, wv_hi, wv_lo, ctx_hi, ctx_lo, v_summed, pairs)

            def unit(g, u, last):
                n, s, b = g * UNITS + u, u % 2, u // UB
                more = not (last and u == UNITS - 1)
                spreads = {(1, 0): 0, (1, 3): 1, (1, 5): 2, (2, 0): 3, (2, 3): 4, (2, 5): 5, (3, 0): 6, (3, 3): 7}
                folds = [{(t, p): 2 * t + p // 4 for t in range(TB) for p in (2, 6)}, {},
                         {(2, 1): 8, (2, 6): 9, (3, 1): 10, (3, 5): 11}, {(t, 4): 12 + t for t in range(TB)}][u]
                if more:
                    sums(n + 1, (u + 1) % 2)
                for t in range(TB):
                    pe.wait_ge(y_added, n * TB + t + 1)
                    for p in range(NP):
                        if more and (t, p) in spreads:
                            spread(n + 1, spreads[t, p])
                        if (t, p) in folds and not (last and u > 0):
                            fold_o(g, folds[t, p])
                        if u == 1 and not last and p % 4 == 2:
                            project(g + 1, [2 * t + p // 4])
                        if t == 0 and p % 2 == 0:
                            pe.wait_ge(p_lo_done, 4 * n + p // 2 + 1 + 8)
                        if t == 0 and u % UB == 0:
                            pe.wait_ge(u_lo_done, g * (2 * NP) + b * NP + p + 1 + 2)
                        cols = slice(t * P, (t + 1) * P)
                        mm = split_product(pe, ps_o[t % 2][:, :], (p_hi[:, s, p, cols], p_lo[:, s, p, cols]),
                                           u_of(b, p), p == 0, p == NP - 1)
                    mm.then_inc(o_summed, 1)

            def group(g, last):
                for u in range(UNITS):
                    unit(g, u, last)

            pe.wait_ge(sum_in, 32)
            sums(0, 0)
            for p in range(NP):
                spread(0, p)
            with pe.Fori(0, NG - 1) as g:
                group(g, False)
            group(NG - 1, True)

        @block.scalar
        def _(act):
            act.sem_inc(v_hi_done, 4)
            act.sem_inc(v32_done, NP)
            act.sem_inc(u_hi_done, NP)

            def exps(n, u, half):
                if not isinstance(n, int) or n >= UB:
                    act.wait_ge(s_in[u % 2], 8 * n - 8 * (u % 2))
                e = s32[:, u % 2, :, :].rearrange("r (a b) t -> r a b t", a=2)[:, :, 2 * half:2 * half + 2, :]
                act.activation(e, e, ACT.Exp, bias=neg_max[:, 0:1]).then_inc(exp_done, 1)

            def round_ctx(g):
                act.wait_ge(ctx_in, 16 * g)
                act.activation(ctx_hi[:, :, :], ctx32[:, :, :], ACT.Copy, scale=CTX_SCALE).then_inc(ctx_hi_done, 1)

            def round_v(g):
                act.wait_ge(v_lo_done, 2 * g)
                act.wait_ge(u_summed, (g - 1) * (2 * NP) + 2 * NP)
                for p in range(NP):
                    if p % 4 == 0:
                        act.wait_ge(v_summed, 2 * g + p // 4 + 1)
                    act.activation(kv32[:, p, :], ps_u[p // 4][:, (p % 4) * KC:(p % 4 + 1) * KC], ACT.Identity,
                                   bias=bkv[:, 1, p:p + 1], scale=1 / (W_SCALE * CTX_SCALE)).then_inc(v32_done, 1)
                act.wait_ge(v32_done, NP * (g + 1))
                round_heads(act, kv_hi, kv32, V_SCALE, v_hi_done)

            def round_u(g, *js):
                for j in js:
                    k, b, p = u_tile(g, j)
                    if j % NP == 0:
                        act.wait_ge(o_summed, g * (UNITS * TB) + (2 * TB if j == 0 else 4 * TB))
                    act.wait_ge(u_summed, k + 1)
                    act.activation(u_of(b, p)[0], ps_u[p % 2][:, :], ACT.Copy,
                                   scale=U_SCALE / (W_SCALE * V_SCALE)).then_inc(u_hi_done, 1)

            def round_r(n):
                act.wait_ge(r_done, n + 1)
                act.activation(r_hi[:, :], r32[:, :], ACT.Copy).then_inc(r_hi_done, 1)
                act.wait_ge(rest_done, n + 1)
                act.activation(r_mid[:, :], rest[:, :], ACT.Copy).then_inc(r_mid_done, 1)

            def round_p(n, s, k):
                if k == 0:
                    act.wait_ge(o_summed, TB * n + TB)
                act.wait_ge(p_scaled, n * NP + 2 * k + 2 + 2)
                act.activation(p_hi[:, s, 2 * k:2 * k + 2, :], s32[:, s, 2 * k:2 * k + 2, :], ACT.Copy)\
                   .then_inc(p_hi_done, 1)

            def group(g, last):
                for u in range(UNITS):
                    n, s = g * UNITS + u, (u + 1) % 2
                    more, more2 = not (last and u == UNITS - 1), not (last and u >= UNITS - 2)
                    halve = lambda k: round_p(n + 1, s, k) if more else None
                    expo = lambda half: exps(n + 2, u, half) if more2 else None
                    fold = lambda *js: round_u(g, *js) if not (last and u > 0) else None
                    if more:
                        round_r(n + 1)
                    if u == 0:
                        fold(0, 1, 2)
                        halve(0)
                        fold(3, 4)
                        halve(1)
                        fold(5)
                        expo(0)
                        fold(6)
                        halve(2)
                        expo(1)
                        fold(7)
                        halve(3)
                        if not last:
                            act.wait_ge(v_summed, 2 * g + 2)
                            round_ctx(g + 1)
                    elif u == 1:
                        halve(0)
                        halve(1)
                        expo(0)
                        halve(2)
                        expo(1)
                        halve(3)
                    elif u == 2:
                        if not last:
                            round_v(g + 1)
                        halve(0)
                        fold(8)
                        halve(1)
                        expo(0)
                        fold(9)
                        halve(2)
                        expo(1)
                        fold(10, 11)
                        halve(3)
                    else:
                        fold(12)
                        halve(0)
                        fold(13)
                        halve(1)
                        fold(14)
                        expo(0)
                        halve(2)
                        expo(1)
                        fold(15)
                        halve(3)

            act.wait_ge(max_done, 1)
            exps(0, 0, 0)
            exps(0, 0, 1)
            exps(1, 1, 0)
            exps(1, 1, 1)
            round_r(0)
            for k in range(4):
                round_p(0, 0, k)
            with act.Fori(0, NG - 1) as g:
                group(g, False)
            group(NG - 1, True)

        @block.vector
        def _(dve):
            dve.sem_inc(u_lo_done, 2 + NP)
            dve.sem_inc(v_lo_done, 2)
            dve.sem_inc(den_done, 1)
            dve.sem_inc(p_scaled, 2)
            dve.sem_inc(p_lo_done, 8)
            dve.sem_inc(y_added, 2)
            dve.sem_inc(ctx_lo_done, 1)

            def split_ctx(g):
                dve.wait_ge(ctx_hi_done, g)
                dve.scalar_tensor_tensor(ctx_lo[:, :, :], ctx32[:, :, :], CTX_SCALE, ctx_hi[:, :, :],
                                         ALU.mult, ALU.subtract).then_inc(ctx_lo_done, 1)

            def split_v(g):
                dve.wait_ge(v_hi_done, 4 * g + 2)
                split_heads(dve, kv_lo, kv_hi, kv32, V_SCALE, v_lo_done)

            def split_u(g, *js):
                for j in js:
                    k, b, p = u_tile(g, j)
                    dve.wait_ge(u_hi_done, k + 1)
                    dve.scalar_tensor_tensor(u_of(b, p)[1], ps_u[p % 2][:, :], U_SCALE / (W_SCALE * V_SCALE),
                                             u_of(b, p)[0], ALU.mult, ALU.subtract).then_inc(u_lo_done, 1)

            def invert(n):
                dve.wait_ge(e_summed, n + 1)
                dve.tensor_scalar(den[:, :], ps_sum[:, 0:HT], TINY, None, ALU.add).then_inc(den_done, 1)
                dve.wait_ge(den_done, n + 2)
                dve.reciprocal(r32[:, :], den[:, :]).then_inc(r_done, 1)

            def second_part(n):
                dve.wait_ge(r_hi_done, n + 1)
                dve.scalar_tensor_tensor(rest[:, :], r_hi[:, :], part[:, 0:1], r32[:, :], ALU.mult, ALU.add)\
                   .then_inc(rest_done, 1)

            def third_part(n):
                dve.wait_ge(r_mid_done, n + 1)
                if not (isinstance(n, int) and n == 0):
                    dve.wait_ge(r_spread, n * NP)
                dve.scalar_tensor_tensor(r_all[:, :], r_mid[:, :], part[:, 1:2], rest[:, :], ALU.mult, ALU.add)\
                   .then_inc(r_all_done, 1)

            def scale_p(n, s, p):
                dve.wait_ge(r_spread, n * NP + p + 1)
                e = s32[:, s, p, :]
                dve.tensor_tensor(e, e, ps_bc[p % 2][:, :], ALU.mult).then_inc(p_scaled, 1)

            def split_p(n, s, k):
                dve.wait_ge(p_hi_done, 4 * n + k + 1)
                at = lambda a: a[:, s, 2 * k:2 * k + 2, :].rearrange("r p t -> r (p t)")
                dve.tensor_tensor(at(p_lo), at(s32), at(p_hi), ALU.subtract).then_inc(p_lo_done, 1)

            def residual(g, u, t):
                n = g * UNITS + u
                k = n * TB + t
                dve.wait_ge(bo_added, k + 1)
                dve.wait_ge(o_summed, k + 1 + 2 * TB)
                y = y32[:, u, t, :]
                dve.scalar_tensor_tensor(y, ps_o[t % 2][:, :], 1 / (P_SCALE * U_SCALE), y, ALU.mult, ALU.add)\
                   .then_inc(y_added, 1)
                dve.wait_ge(y_added, k + 3)
                dve.bn_stats(stats[:, t, :], y)
                dve.drain()
                dve.bn_aggr(mean_var[:, t, :], stats[:, t, :]).then_inc(mean_done, 1)

            def norm(g, u, t):
                dve.wait_ge(rstd_done, (g * UNITS + u) * TB + t + 1)
                y = y32[:, u, t, :]
                dve.tensor_scalar(y, y, mean_var[:, t, 0:1], rstd[:, t:t + 1], ALU.subtract, ALU.mult)\
                   .then_inc(normed, 1)

            def group(g, last):
                for u in range(UNITS):
                    n, s = g * UNITS + u + 1, (u + 1) % 2
                    more = not (last and u == UNITS - 1)
                    scale = lambda *ps: [scale_p(n, s, p) for p in ps] if more else None
                    split = lambda *ks: [split_p(n, s, k) for k in ks] if more else None
                    fold = lambda *js: split_u(g, *js) if not (last and u > 0) else None
                    more2 = not (last and u >= UNITS - 2)
                    if more:
                        third_part(n)
                    if u == 0:
                        fold(0, 1)
                        residual(g, u, 0)
                        scale(0)
                        fold(2)
                        scale(1, 2)
                        split(0)
                        fold(3)
                        residual(g, u, 1)
                        norm(g, u, 0)
                        scale(3)
                        fold(4)
                        scale(4)
                        split(1)
                        scale(5)
                        fold(5)
                        residual(g, u, 2)
                        norm(g, u, 1)
                        scale(6)
                        fold(6)
                        scale(7)
                        split(2, 3)
                        fold(7)
                        if not last:
                            split_ctx(g + 1)
                    elif u == 1:
                        residual(g, u, 0)
                        scale(0, 1, 2)
                        split(0)
                        residual(g, u, 1)
                        norm(g, u, 0)
                        scale(3, 4)
                        split(1)
                        scale(5)
                        residual(g, u, 2)
                        norm(g, u, 1)
                        scale(6, 7)
                        split(2, 3)
                    elif u == 2:
                        residual(g, u, 0)
                        scale(0, 1)
                        if not last:
                            split_v(g + 1)
                        scale(2)
                        split(0)
                        residual(g, u, 1)
                        norm(g, u, 0)
                        scale(3, 4)
                        fold(8)
                        split(1)
                        scale(5)
                        fold(9)
                        residual(g, u, 2)
                        norm(g, u, 1)
                        scale(6, 7)
                        fold(10)
                        split(2)
                        fold(11)
                        split(3)
                    else:
                        fold(12)
                        residual(g, u, 0)
                        scale(0, 1)
                        fold(13)
                        scale(2)
                        split(0)
                        residual(g, u, 1)
                        norm(g, u, 0)
                        scale(3, 4)
                        split(1)
                        fold(14)
                        scale(5)
                        residual(g, u, 2)
                        norm(g, u, 1)
                        scale(6, 7)
                        split(2)
                        fold(15)
                        split(3)
                    residual(g, u, 3)
                    if more2:
                        invert(n + 1)
                    norm(g, u, 2)
                    if more2:
                        second_part(n + 1)
                    norm(g, u, 3)

            dve.tensor_scalar(key_max[:, :], least[:, :], -1.0, MASKED, ALU.mult, ALU.add).then_inc(key_max_done, 1)
            dve.wait_ge(key_max_done, 1)
            dve.tensor_tensor(score_max[:, :], score_max[:, :], key_max[:, :], ALU.max).then_inc(max_local, 1)
            dve.wait_ge(max_global, 1)
            dve.tensor_scalar(neg_max[:, :], key_max[:, :], -1.0, None, ALU.mult).then_inc(max_done, 1)
            dve.wait_ge(sum_in, 32)
            invert(0)
            second_part(0)
            third_part(0)
            for p in range(NP):
                scale_p(0, 0, p)
                if p in (3, 5):
                    split_p(0, 0, p // 2 - 1)
            split_p(0, 0, 2)
            split_p(0, 0, 3)
            invert(1)
            second_part(1)
            with dve.Fori(0, NG - 1) as g:
                group(g, False)
            group(NG - 1, True)

        @block.gpsimd
        def _(pool):
            pool.wait_ge(max_local, 1)
            pool.partition_all_reduce(key_max[:, :], score_max[:, :], P, bass.bass_isa.ReduceOp.max)\
                .then_inc(max_global, 1)
            pool.memset(minus_half[:, :], -0.5).then_inc(consts_done, 1)
            pool.memset(ln_eps[:, :], LN_EPS).then_inc(consts_done, 1)
            pool.wait_ge(consts_done, 2)
            pool.wait_ge(affine_in, 48)

            def add_bo(g, u, t):
                s = u % UNITS
                if t == 0:
                    pool.wait_ge(x_in[s], 16 * g + 16 * (u // UNITS) + 16)
                y = y32[:, s, t, :]
                pool.tensor_tensor(y, y, bo_b[:, :], ALU.add).then_inc(bo_added, 1)

            def inv_std(g, u, t):
                k = (g * UNITS + u) * TB + t + 1
                pool.wait_ge(mean_done, k)
                pool.tensor_tensor(var_eps[:, t:t + 1], mean_var[:, t, 1:2], ln_eps[:, :], ALU.add)\
                    .then_inc(eps_added, 1)
                pool.wait_ge(eps_added, k)
                pool.tensor_tensor(rstd[:, t:t + 1], var_eps[:, t:t + 1], minus_half[:, :], ALU.pow)\
                    .then_inc(rstd_done, 1)

            def affine(g, u, t):
                k = (g * UNITS + u) * TB + t + 1
                y = y32[:, u, t, :]
                pool.wait_ge(normed, k)
                pool.tensor_tensor(y, y, gamma_b[:, :], ALU.mult).then_inc(scaled, 1)
                pool.wait_ge(scaled, k)
                pool.tensor_tensor(y, y, beta_b[:, :], ALU.add).then_inc(shifted, 1)

            def group(g, last):
                for u in range(UNITS):
                    for t in range(TB):
                        inv_std(g, u, t)
                        if t > 0:
                            affine(g, u, t - 1)
                        if not (last and u == UNITS - 1):
                            add_bo(g, u + 1, t)
                    affine(g, u, TB - 1)

            for t in range(TB):
                add_bo(0, 0, t)
            with pool.Fori(0, NG - 1) as g:
                group(g, False)
            group(NG - 1, True)


def kernel(**inputs):
    import numpy as np
    import concourse.bacc as bacc
    from concourse.bass_utils import run_bass_kernel_spmd

    a = {k.removeprefix("L0_xattn_"): np.asarray(v) for k, v in inputs.items()}

    def columns(v):
        return v.reshape(-1, P).T

    sel_sum = np.zeros((P, NP // 2, 32), np.float32)
    sel_bc = np.zeros((P, NP, 2, P), np.float32)
    part = np.zeros((P, 2), np.float32)
    for k in range(COPIES):
        for h in range(2):
            for p in range(NP):
                row, keys = 8 * k + 2 * (p % 4) + h, slice(h * NK, (h + 1) * NK)
                sel_sum[keys, p % 4, row] = 1.0
                for th in range(2):
                    q = 2 * th + p // 4
                    sel_bc[32 * q + row, p, th, keys] = P_SCALE
                    part[32 * q + row] = (-1.0 if k >= 1 else 0.0, -1.0 if k >= 2 else 0.0)

    turned = np.roll(np.arange(B), -1)
    context = a["ctx_1024"].transpose(2, 0, 1).reshape(DC, P, B, NK)
    arrays = {
        "xT": a["x"].transpose(0, 2, 1).reshape(B, DC, P, T)[turned],
        "x": a["x"],
        "ctxT": context.reshape(DC, P, B * NK),
        "ctxT_turned": context[:, :, [*turned, *range(GB)]].reshape(DC, P, (B + GB) * NK),
        "maskT": a["mask_BxSxS2_ik1"].transpose(0, 2, 1)[turned],
        "wk": a["Wk"].reshape(DC, P, HD),
        "wqT": a["Wq"].T.reshape(4, 2, P, D).transpose(0, 2, 1, 3).reshape(4, P, 2 * D),
        "wv": a["Wv"].reshape(DC, P, HD),
        "wo": a["Wo"].reshape(4, 2, P, D).transpose(0, 2, 1, 3).reshape(4, P, 2 * D),
        "bk": columns(a["bk"]), "bq": columns(a["bq"]), "bv": columns(a["bv"]),
        "bo": a["bo"], "gamma": a["gamma"], "beta": a["beta"],
        "sel_sum": sel_sum, "sel_bc": sel_bc.reshape(P, 2, -1).transpose(1, 0, 2), "part": part,
    }
    nc = bacc.Bacc("TRN2", target_bir_lowering=False, num_devices=1)
    aps = {}
    for name, v in arrays.items():
        arrays[name] = v = np.ascontiguousarray(v)
        aps[name] = nc.dram_tensor(name + "_in", v.shape, mybir.dt.from_np(v.dtype), kind="ExternalInput").ap()
    out = nc.dram_tensor("out", (B, T, D), F32, kind="ExternalOutput").ap()
    build(nc, *(aps[k] for k in ("xT", "x", "ctxT", "ctxT_turned", "maskT", "wk", "wqT", "wv", "wo", "bk", "bq", "bv",
                                 "bo", "gamma", "beta", "sel_sum", "sel_bc", "part")), out)
    r = run_bass_kernel_spmd(nc, [{name + "_in": v for name, v in arrays.items()}], core_ids=[0])
    return r.results[0]["out"]
```
